# Optimizing a Trainium2 kernel written in Bass

```python
import numpy as np
import jax
import jax.numpy as jnp

def _softmax(x, axis=-1):
    return jax.nn.softmax(x, axis=axis)

def _gelu(x):
    return jax.nn.gelu(x, approximate=True)

def _silu(x):
    return jax.nn.silu(x)

def _sigmoid(x):
    return jax.nn.sigmoid(x)

def _layernorm(x, axis=-1, eps=1e-05):
    m = jnp.mean(x, axis=axis, keepdims=True)
    v = jnp.var(x, axis=axis, keepdims=True)
    return (x - m) / jnp.sqrt(v + eps)

def _scatter_add(tgt, idx, src, axis=0):
    return tgt.at[idx].add(src)

def _segment_sum(src, seg, n):
    return jax.ops.segment_sum(src, seg, n)
kernel_name = 'mk_metaformer_d2_conv_nchw128_r4_e8d652'

def setup_inputs(seed: int=0):
    np.random.seed(seed)
    _w = jnp.asarray

    def _rec_inputs():
        import jax
        import jax.numpy as jnp
        _gk = jax.random.key(seed)
        x = -7.109e-05 + 0.9999 * jax.random.normal(jax.random.fold_in(_gk, 1), (8, 32, 64, 64), jnp.float32)
        return x
    x = _rec_inputs()

    def _L0_conv_setup():
        import jax, jax.numpy as jnp
        import numpy as np
        B, CIN, COUT, H, W = (8, 32, 32, 64, 64)
        HM0, HM1 = (32, 32)
        W_SCALE = 1.0 / (CIN * COUT)
        key = jax.random.key(seed)
        kx, k1r, k1i, k2r, k2i = jax.random.split(key, 5)
        x = jax.random.normal(kx, (B, CIN, H, W), dtype=jnp.float32)
        w1_real = jax.random.normal(k1r, (CIN, COUT, HM0, HM1), dtype=jnp.float32) * W_SCALE
        w1_imag = jax.random.normal(k1i, (CIN, COUT, HM0, HM1), dtype=jnp.float32) * W_SCALE
        w2_real = jax.random.normal(k2r, (CIN, COUT, HM0, HM1), dtype=jnp.float32) * W_SCALE
        w2_imag = jax.random.normal(k2i, (CIN, COUT, HM0, HM1), dtype=jnp.float32) * W_SCALE
        return {'x': x, 'w1_real': w1_real, 'w1_imag': w1_imag, 'w2_real': w2_real, 'w2_imag': w2_imag}
    _L0_conv_all = _L0_conv_setup()
    _L0_conv_in = {k: v for k, v in _L0_conv_all.items() if k in ('w1_real', 'w1_imag', 'w2_real', 'w2_imag')}
    del _L0_conv_all

    def _L0_ffn_setup():
        import jax, jax.numpy as jnp
        import numpy as np
        B, S, D, E, H, O, K = (128, 512, 32, 16, 128, 32, 8)
        key = jax.random.key(seed)
        k0, k1, k2, k3 = jax.random.split(key, 4)
        x = jax.random.normal(k0, (B, S, D), dtype=jnp.float32)
        gate_w = jax.random.normal(k1, (E, D), dtype=jnp.float32) * (1.0 / np.sqrt(D))
        gate_b = jnp.zeros((E,), dtype=jnp.float32)
        weight1 = jax.random.uniform(k2, (E, D + 1, H), dtype=jnp.float32, minval=-1.0, maxval=1.0) * (1.0 / np.sqrt(D + 1))
        weight2 = jax.random.uniform(k3, (E, H + 1, O), dtype=jnp.float32, minval=-1.0, maxval=1.0) * (1.0 / np.sqrt(H + 1))
        return {'x': x, 'gate_w': gate_w, 'gate_b': gate_b, 'weight1': weight1, 'weight2': weight2}
    _L0_ffn_all = _L0_ffn_setup()
    _L0_ffn_in = {k: v for k, v in _L0_ffn_all.items() if k in ('gate_w', 'gate_b', 'weight1', 'weight2')}
    del _L0_ffn_all

    def _L1_conv_setup():
        import jax, jax.numpy as jnp
        import numpy as np
        import math
        C = 32
        KSIZE = 9
        PAD = KSIZE // 2

        def _conv1d(v, w, b):
            y = jax.lax.conv_general_dilated(v, w, window_strides=(1,), padding=[(PAD, PAD)], dimension_numbers=('NCH', 'OIH', 'NCH'))
            return y + b[None, :, None]

        def _sweep(x, w, b, axis, reverse):
            rows = jnp.moveaxis(x, axis, 0)
            if reverse:
                rows = rows[::-1]

            def step(prev, row):
                new = row + jax.nn.relu(_conv1d(prev, w, b))
                return (new, new)
            _, rest = jax.lax.scan(step, rows[0], rows[1:])
            out = jnp.concatenate([rows[:1], rest], axis=0)
            if reverse:
                out = out[::-1]
            return jnp.moveaxis(out, 0, axis)
        key = jax.random.key(seed)
        ks = jax.random.split(key, 9)
        B, H, W = (32, 18, 50)
        bound = math.sqrt(2.0 / (C * 9 * 5))
        x = jax.random.normal(ks[0], (B, C, H, W), dtype=jnp.float32)

        def wgt(k):
            return jax.random.uniform(k, (C, C, KSIZE), dtype=jnp.float32, minval=-bound, maxval=bound)

        def bia(k):
            return 0.01 * jax.random.normal(k, (C,), dtype=jnp.float32)
        return {'x': x, 'w_d': wgt(ks[1]), 'b_d': bia(ks[2]), 'w_u': wgt(ks[3]), 'b_u': bia(ks[4]), 'w_r': wgt(ks[5]), 'b_r': bia(ks[6]), 'w_l': wgt(ks[7]), 'b_l': bia(ks[8])}
    _L1_conv_all = _L1_conv_setup()
    _L1_conv_in = {k: v for k, v in _L1_conv_all.items() if k in ('w_d', 'b_d', 'w_u', 'b_u', 'w_r', 'b_r', 'w_l', 'b_l')}
    del _L1_conv_all

    def _L1_ffn_setup():
        import jax, jax.numpy as jnp
        import numpy as np
        B, S, D, E, H, O, K = (128, 512, 32, 16, 128, 32, 8)
        key = jax.random.key(seed)
        k0, k1, k2, k3 = jax.random.split(key, 4)
        x = jax.random.normal(k0, (B, S, D), dtype=jnp.float32)
        gate_w = jax.random.normal(k1, (E, D), dtype=jnp.float32) * (1.0 / np.sqrt(D))
        gate_b = jnp.zeros((E,), dtype=jnp.float32)
        weight1 = jax.random.uniform(k2, (E, D + 1, H), dtype=jnp.float32, minval=-1.0, maxval=1.0) * (1.0 / np.sqrt(D + 1))
        weight2 = jax.random.uniform(k3, (E, H + 1, O), dtype=jnp.float32, minval=-1.0, maxval=1.0) * (1.0 / np.sqrt(H + 1))
        return {'x': x, 'gate_w': gate_w, 'gate_b': gate_b, 'weight1': weight1, 'weight2': weight2}
    _L1_ffn_all = _L1_ffn_setup()
    _L1_ffn_in = {k: v for k, v in _L1_ffn_all.items() if k in ('gate_w', 'gate_b', 'weight1', 'weight2')}
    del _L1_ffn_all
    return {'x': x, 'L0_conv_w1_real': _L0_conv_in['w1_real'], 'L0_conv_w1_imag': _L0_conv_in['w1_imag'], 'L0_conv_w2_real': _L0_conv_in['w2_real'], 'L0_conv_w2_imag': _L0_conv_in['w2_imag'], 'L0_ffn_gate_w': _L0_ffn_in['gate_w'], 'L0_ffn_gate_b': _L0_ffn_in['gate_b'], 'L0_ffn_weight1': _L0_ffn_in['weight1'], 'L0_ffn_weight2': _L0_ffn_in['weight2'], 'L1_conv_w_d': _L1_conv_in['w_d'], 'L1_conv_b_d': _L1_conv_in['b_d'], 'L1_conv_w_u': _L1_conv_in['w_u'], 'L1_conv_b_u': _L1_conv_in['b_u'], 'L1_conv_w_r': _L1_conv_in['w_r'], 'L1_conv_b_r': _L1_conv_in['b_r'], 'L1_conv_w_l': _L1_conv_in['w_l'], 'L1_conv_b_l': _L1_conv_in['b_l'], 'L1_ffn_gate_w': _L1_ffn_in['gate_w'], 'L1_ffn_gate_b': _L1_ffn_in['gate_b'], 'L1_ffn_weight1': _L1_ffn_in['weight1'], 'L1_ffn_weight2': _L1_ffn_in['weight2']}

def reference(x, L0_conv_w1_real, L0_conv_w1_imag, L0_conv_w2_real, L0_conv_w2_imag, L0_ffn_gate_w, L0_ffn_gate_b, L0_ffn_weight1, L0_ffn_weight2, L1_conv_w_d, L1_conv_b_d, L1_conv_w_u, L1_conv_b_u, L1_conv_w_r, L1_conv_b_r, L1_conv_w_l, L1_conv_b_l, L1_ffn_gate_w, L1_ffn_gate_b, L1_ffn_weight1, L1_ffn_weight2):
    import jax
    import jax.numpy as jnp

    def _L0_conv_ref(x, w1_real, w1_imag, w2_real, w2_imag):
        import jax, jax.numpy as jnp
        import numpy as np
        B, CIN, COUT, H, W = (8, 32, 32, 64, 64)
        HM0, HM1 = (32, 32)
        W_SCALE = 1.0 / (CIN * COUT)
        "2D FactorizedSpectralConv forward (dense weights, separable=False, no bias).\n\n            rfft2 (norm='forward') -> contract two low-frequency corners with complex\n            weights via einsum 'bixy,ioxy->boxy' -> zero-fill remaining modes -> irfft2.\n            "
        b, cin, h, w = x.shape
        cout = w1_real.shape[1]
        hm0, hm1 = (w1_real.shape[2], w1_real.shape[3])
        xf = jnp.fft.rfft2(x, norm='forward')
        w1 = jax.lax.complex(w1_real, w1_imag)
        w2 = jax.lax.complex(w2_real, w2_imag)
        top = jnp.einsum('bixy,ioxy->boxy', xf[:, :, :hm0, :hm1], w1)
        bot = jnp.einsum('bixy,ioxy->boxy', xf[:, :, -hm0:, :hm1], w2)
        out_fft = jnp.zeros((b, cout, h, w // 2 + 1), dtype=xf.dtype)
        out_fft = out_fft.at[:, :, :hm0, :hm1].set(top)
        out_fft = out_fft.at[:, :, -hm0:, :hm1].set(bot)
        return jnp.fft.irfft2(out_fft, s=(h, w), norm='forward')

    def _L0_ffn_ref(x, gate_w, gate_b, weight1, weight2):
        import jax, jax.numpy as jnp
        import numpy as np
        B, S, D, E, H, O, K = (128, 512, 32, 16, 128, 32, 8)
        Bn, Sn, Dn = x.shape
        logits = jnp.einsum('bsd,ed->bse', x, gate_w) + gate_b
        probs = jax.nn.softmax(logits, axis=1)
        vals, idx = jax.lax.top_k(probs.transpose(0, 2, 1), K)
        topv = vals.transpose(0, 2, 1)
        topi = idx.transpose(0, 2, 1)
        flat_idx = topi.reshape(Bn, K * E)
        gathered = jnp.take_along_axis(x, flat_idx[:, :, None], axis=1)
        gathered = gathered.reshape(Bn, K, E, Dn)
        pooled = jnp.einsum('bked,bke->bed', gathered, topv)
        ones = jnp.ones((E, Bn, 1), dtype=x.dtype)
        h = jnp.concatenate([pooled.transpose(1, 0, 2), ones], axis=-1)
        h = jax.nn.gelu(jnp.einsum('ebd,edh->ebh', h, weight1), approximate=False)
        h = jnp.concatenate([h, ones], axis=-1)
        out = jnp.einsum('ebh,eho->ebo', h, weight2)
        out = out.transpose(1, 0, 2)
        weighted = jnp.einsum('beo,bke->bkeo', out, topv).reshape(Bn, K * E, O)
        outputs = jnp.zeros((Bn, Sn, O), dtype=x.dtype)
        outputs = outputs.at[jnp.arange(Bn)[:, None], flat_idx].add(weighted)
        return outputs

    def _L1_conv_ref(x, w_d, b_d, w_u, b_u, w_r, b_r, w_l, b_l):
        import jax, jax.numpy as jnp
        import numpy as np
        import math
        C = 32
        KSIZE = 9
        PAD = KSIZE // 2

        def _conv1d(v, w, b):
            y = jax.lax.conv_general_dilated(v, w, window_strides=(1,), padding=[(PAD, PAD)], dimension_numbers=('NCH', 'OIH', 'NCH'))
            return y + b[None, :, None]

        def _sweep(x, w, b, axis, reverse):
            rows = jnp.moveaxis(x, axis, 0)
            if reverse:
                rows = rows[::-1]

            def step(prev, row):
                new = row + jax.nn.relu(_conv1d(prev, w, b))
                return (new, new)
            _, rest = jax.lax.scan(step, rows[0], rows[1:])
            out = jnp.concatenate([rows[:1], rest], axis=0)
            if reverse:
                out = out[::-1]
            return jnp.moveaxis(out, 0, axis)
        out = _sweep(x, w_d, b_d, axis=2, reverse=False)
        out = _sweep(out, w_u, b_u, axis=2, reverse=True)
        out = _sweep(out, w_r, b_r, axis=3, reverse=False)
        out = _sweep(out, w_l, b_l, axis=3, reverse=True)
        return out

    def _L1_ffn_ref(x, gate_w, gate_b, weight1, weight2):
        import jax, jax.numpy as jnp
        import numpy as np
        B, S, D, E, H, O, K = (128, 512, 32, 16, 128, 32, 8)
        Bn, Sn, Dn = x.shape
        logits = jnp.einsum('bsd,ed->bse', x, gate_w) + gate_b
        probs = jax.nn.softmax(logits, axis=1)
        vals, idx = jax.lax.top_k(probs.transpose(0, 2, 1), K)
        topv = vals.transpose(0, 2, 1)
        topi = idx.transpose(0, 2, 1)
        flat_idx = topi.reshape(Bn, K * E)
        gathered = jnp.take_along_axis(x, flat_idx[:, :, None], axis=1)
        gathered = gathered.reshape(Bn, K, E, Dn)
        pooled = jnp.einsum('bked,bke->bed', gathered, topv)
        ones = jnp.ones((E, Bn, 1), dtype=x.dtype)
        h = jnp.concatenate([pooled.transpose(1, 0, 2), ones], axis=-1)
        h = jax.nn.gelu(jnp.einsum('ebd,edh->ebh', h, weight1), approximate=False)
        h = jnp.concatenate([h, ones], axis=-1)
        out = jnp.einsum('ebh,eho->ebo', h, weight2)
        out = out.transpose(1, 0, 2)
        weighted = jnp.einsum('beo,bke->bkeo', out, topv).reshape(Bn, K * E, O)
        outputs = jnp.zeros((Bn, Sn, O), dtype=x.dtype)
        outputs = outputs.at[jnp.arange(Bn)[:, None], flat_idx].add(weighted)
        return outputs

    def _gn(v, G=32, eps=1e-05):
        B_, C_, H_, W_ = v.shape
        g = v.reshape(B_, G, C_ // G, H_, W_)
        m = jnp.mean(g, axis=(2, 3, 4), keepdims=True)
        s = jnp.var(g, axis=(2, 3, 4), keepdims=True)
        return ((g - m) / jnp.sqrt(s + eps)).reshape(v.shape)

    def _ln_c(v, eps=1e-06):
        m = jnp.mean(v, axis=1, keepdims=True)
        s = jnp.var(v, axis=1, keepdims=True)
        return (v - m) / jnp.sqrt(s + eps)

    def _ln_t(v, eps=1e-05):
        m = jnp.mean(v, axis=-1, keepdims=True)
        s = jnp.var(v, axis=-1, keepdims=True)
        return (v - m) / jnp.sqrt(s + eps)

    def _to_tokens(v):
        B_, C_, H_, W_ = v.shape
        return v.reshape(B_, C_, H_ * W_).transpose(0, 2, 1)

    def _from_tokens(t, like):
        B_, C_, H_, W_ = like.shape
        return t.transpose(0, 2, 1).reshape(B_, C_, H_, W_)
    x = x + _L0_conv_ref(_ln_c(x), L0_conv_w1_real, L0_conv_w1_imag, L0_conv_w2_real, L0_conv_w2_imag)
    t = _to_tokens(x)
    t = t + _L0_ffn_ref(_ln_t(t), L0_ffn_gate_w, L0_ffn_gate_b, L0_ffn_weight1, L0_ffn_weight2)
    x = _from_tokens(t, x)
    x = x + _L1_conv_ref(_ln_c(x), L1_conv_w_d, L1_conv_b_d, L1_conv_w_u, L1_conv_b_u, L1_conv_w_r, L1_conv_b_r, L1_conv_w_l, L1_conv_b_l)
    t = _to_tokens(x)
    t = t + _L1_ffn_ref(_ln_t(t), L1_ffn_gate_w, L1_ffn_gate_b, L1_ffn_weight1, L1_ffn_weight2)
    x = _from_tokens(t, x)
    return x

_drawn_inputs = setup_inputs


def setup_inputs(seed=0):
    import zlib

    import numpy as np

    out = dict(_drawn_inputs(seed))
    spreads = {'L0_ffn_gate_b': (0.0, 0.8), 'L1_ffn_gate_b': (0.0, 0.1)}
    factors = {'L0_conv_w1_real': 8.0,
     'L0_conv_w1_imag': 8.0,
     'L0_conv_w2_real': 8.0,
     'L0_conv_w2_imag': 8.0,
     'L0_ffn_gate_w': 8.0,
     'L0_ffn_weight1': 8.0,
     'L0_ffn_weight2': 8.0,
     'L1_conv_b_d': 8.0,
     'L1_conv_b_u': 8.0,
     'L1_conv_b_r': 8.0,
     'L1_conv_b_l': 8.0,
     'L1_ffn_gate_w': 8.0,
     'L1_ffn_weight1': 8.0,
     'L1_ffn_weight2': 8.0}
    for name, (base, spread) in spreads.items():
        noise = np.random.default_rng([zlib.crc32(name.encode()), seed]).standard_normal(out[name].shape)
        drawn = base * np.exp(spread * noise) if base else spread * noise
        out[name] = jnp.asarray(drawn.astype(out[name].dtype))
    for name, factor in factors.items():
        out[name] = (out[name] * factor).astype(out[name].dtype)
    return out
```

```python
from contextlib import ExitStack

import numpy as np

import concourse.bass as bass
from concourse import mybir

B, C, H, W = 8, 32, 64, 64
P = 128
BL, BH = P // C, B * C // P
TOK = H * W
KY = W // 2
NE, NHID = 16, 128
Q = 4
HO = H // Q
TAPS = 9
NT = TOK // P
BANK = 512
KYC = 4
NCH = KY // KYC
X8 = H // 2 // Q
WCOLS = 2 * X8 * KYC * 2 * C
NF = BH * TOK
LN_C_EPS, LN_T_EPS = (1e-6, 1e-6), 1e-5
MASKED = -3.0e38

F32 = mybir.dt.float32
BF16 = mybir.dt.bfloat16
ALU = mybir.AluOpType
ACT = mybir.ActivationFunctionType
AX_X = mybir.AxisListType.X


def build_kernel(nc, x_in, dft, wspec, conv_w, conv_b, gate_w, gate_b, w1, w2, b2, own, out):
    with ExitStack() as ctx:
        def sb(name, shape, dt=F32):
            return ctx.enter_context(nc.sbuf_tensor(name, shape, dt))

        def sem(name):
            return ctx.enter_context(nc.semaphore(name))

        RA, RB, RCD = sb("RA", [P, NF]), sb("RB", [P, NF]), sb("RCD", [P, 2 * NF])
        RC, RD = RCD[:, 0:NF], RCD[:, NF:2 * NF]
        RE = sb("RE", [P, 3 * WCOLS])
        PS = ctx.enter_context(nc.psum_tensor("PS", [P, 8, BANK], F32))

        dft_sb = sb("dft_sb", [P, 6, P])
        centre, ident, fwd_w, fwd_h, inv_h, inv_w = (dft_sb[:, i, :] for i in range(6))
        own_sb = sb("own_sb", [P, B])
        conv_sb = sb("conv_sb", [P, 4, 3, P])
        convb_sb, negb_sb = sb("convb_sb", [P, 4]), sb("negb_sb", [P, 4])
        gate_sb = sb("gate_sb", [P, 2, BL * NE])
        proj = sb("proj", [P, 2, P + BL * NE])
        gateb_sb = sb("gateb_sb", [P, 2])
        w1_sb = sb("w1_sb", [C + 1, NE, NHID])
        w2_sb, b2_sb = sb("w2_sb", [P, 2, NE, C]), sb("b2_sb", [C, 2, NE])
        eps_sb = sb("eps_sb", [P, 2])
        sums, std, rstd = sb("sums", [P, 256]), sb("std", [P, 256]), sb("rstd", [P, 256])
        top8 = sb("top8", [P, 8])
        negmax, expsum, rsum = sb("negmax", [P, 1]), sb("expsum", [P, 1]), sb("rsum", [P, 1])
        ones = sb("ones", [1, C])
        rs_row, rs_rep = sb("rs_row", [1, P]), sb("rs_rep", [C, P])
        pooled = sb("pooled", [C + 1, B, NE])
        hid = sb("hid", [P, NE, B])
        eout = sb("eout", [C, B, NE])
        espread = sb("espread", [P, B, C])
        state = sb("state", [P, 2, B, HO + 2])
        warm = sb("warm", [P, P], BF16)

        s_x = [sem(f"x_loaded{i}") for i in range(4)]
        s_dft, s_par = sem("dft_loaded"), sem("params_loaded")
        s_w1 = [sem(f"w1_loaded{i}") for i in range(2)]
        s_wc = [sem(f"wspec_loaded{i}") for i in range(3)]
        s_xr = sem("x_reloaded")
        s_set, s_zero = sem("memsets_done"), sem("xb_zeroed")
        s_gp, s_gpc = sem("gate_projected"), sem("gate_copied")
        s_cen, s_sq, s_sum = sem("ln_centred"), sem("squared"), sem("summed")
        s_std, s_rec, s_nrm = sem("std_ready"), sem("rstd_ready"), sem("ln_normed")
        s_full, s_da, s_dd = sem("group_full"), sem("group_drained_act"), sem("group_drained_dve")
        s_f2, s_xba, s_xbd = sem("spectrum_full"), sem("xb_written_act"), sem("xb_written_dve")
        s_mix, s_ma, s_md = sem("mixed"), sem("mix_drained_act"), sem("mix_drained_dve")
        s_t0, s_t1 = sem("products_re_turned"), sem("products_im_turned")
        s_tmp, s_comb = sem("products_im_copied"), sem("products_combined")
        s_if1, s_res = sem("image_full"), sem("residual_added")
        s_pr, s_xc, s_lg = sem("projected"), sem("centred_copied"), sem("logits_scaled")
        s_mx, s_nm, s_rep = sem("top8_found"), sem("negmax_ready"), sem("top8_replaced")
        s_exp, s_rs, s_msk = sem("exps_ready"), sem("rsum_ready"), sem("weights_masked")
        s_ord = sem("weights_ordered")
        s_wt, s_wtd = sem("weights_turned"), sem("weights_scaled")
        s_rt, s_rr = sem("rsum_turned"), sem("rsum_row_copied")
        s_rb, s_rp = sem("rsum_spread"), sem("rsum_rep_copied")
        s_pl, s_pc = sem("pooled_full"), sem("pooled_copied")
        s_h, s_g = sem("hidden_full"), sem("gelu_done")
        s_o, s_ob = sem("experts_full"), sem("experts_biased")
        s_ot, s_os = sem("experts_turned"), sem("experts_spread")
        s_sc, s_ad = sem("scatter_full"), sem("scatter_added")
        s_pw = [sem(f"rows_in{i}") for i in range(BH)]
        s_st, s_cv = sem("state_ready"), sem("conv_ready")
        s_row, s_arc = sem("row_fetched"), sem("row_archived")
        s_ph = sem("columns_in")
        s_co = [sem(f"conv_out{i}") for i in range(Q)]
        s_x3, s_out = sem("conv_added"), sem("stored")
        N_SET, N_PAR = 6, 7

        def blk(region, n):
            return region[:, n * P:(n + 1) * P]

        def banks(b0, nb):
            return PS[:, b0:b0 + nb, :].rearrange("p k c -> p (k c)")

        XB = RB[:, :].rearrange("p (s x z r q b) -> p s x z r q b", s=2, x=X8, z=2 * KYC, r=2, q=Q)
        Z = RCD[:, :].rearrange("p (c x w n) -> p c x w n", c=NCH, x=X8, w=2)
        V = RA[:, :].rearrange("p (c x a r n) -> p c x a r n", c=NCH, x=X8, a=2, r=2)
        V_of_b = RA[:, :].rearrange("p (c m b) -> p c m b", c=NCH, b=B)
        WR = RE[:, :].rearrange("p (s a x y n) -> p s a x y n", s=3, a=2, x=X8, y=KYC)
        imtmp = RE[:, 0:2 * 1024].rearrange("p (s n) -> p s n", s=2)
        square = RE[:, 2 * WCOLS:3 * WCOLS].rearrange("p (s n) -> p s n", s=2)
        LT = RD[:, 0:TOK].rearrange("p (t h n) -> p t h n", h=BH, t=NT)
        L = (RB[:, 0:TOK], RC[:, 0:TOK])
        L2, E = RD[:, 0:TOK], RD[:, TOK:2 * TOK]
        WTOK = RE[:, 0:WCOLS].rearrange("p (t n) -> p t n", t=NT)
        XH = RB[:, :].rearrange("p (j i t o v) -> p j i t o v", j=Q, i=Q, t=BH, o=HO)
        XW = RD.rearrange("p (i b o v) -> p i b o v", i=Q, b=B, o=HO)
        XV = RE[:, 0:NF].rearrange("p (j b o v) -> p j b o v", j=Q, b=B, o=HO)
        CO = RA[:, :].rearrange("p (i j t o v) -> p i j t o v", i=Q, j=Q, t=BH, o=HO)
        X3 = RB[:, :].rearrange("p (i j t o v) -> p i j t o v", i=Q, j=Q, t=BH, o=HO)

        rowb = RA[:, 0:4 * P].rearrange("p (s b v) -> p s b v", s=4, b=B)

        def by_position(ap):
            return ap.rearrange("p (o i v j) -> p i j o v", i=Q, v=HO, j=Q)

        G_F1, G_T1, G_T2, G_IF2, G_T3, G_TB = 0, 8, 16, 24, 32, 44
        G_LT = (40, 52)
        LN0, EX0 = (0, 12), (4, 16)

        def slot(j):
            return banks(2 * (j % 4), 2)

        def wait_drained(eng, j):
            eng.wait_ge(s_da, j // 2 + 1)
            if j >= 1:
                eng.wait_ge(s_dd, (j + 1) // 2)

        def wait_one_drained(eng, j):
            eng.wait_ge(s_dd if j % 2 else s_da, j // 2 + 1)

        def f1_pairs(j):
            g = j - G_F1
            o = RC.rearrange("p (t k r h) -> p t h r k", t=BH, k=KY, r=2)[:, g // 4, 16 * (g % 4):16 * (g % 4) + 16]
            return [(o, slot(j).rearrange("p (h r k) -> p h r k", r=2, k=KY))]

        def t1_pairs(j):
            g = j - G_T1
            return [(RA[:, 1024 * g:1024 * g + 1024], slot(j))]

        def xb_pairs(c, bh):
            pairs = []
            for bl in range(BL):
                for q in range(Q):
                    i = PS[C * bl:C * bl + C, 2 * (c % 2) + bh, :].rearrange("p (z q r x) -> p q z r x", q=Q, r=2, x=X8)
                    o = XB[C * q:C * q + C, c % 2, :, :, :, q, bh * BL + bl].rearrange("p x z r -> p z r x")
                    pairs.append((o, i[:, q]))
            return pairs

        def z_bank(c, k):
            return RCD[:, 2048 * c + BANK * k:2048 * c + BANK * (k + 1)]

        def t2_pairs(j):
            c = j - G_T2
            pairs = []
            for bh in range(BH):
                o = RB[:, :].rearrange("p (t k b o) -> p t b k o", t=BH, k=KY, b=BL)[:, bh, :, KYC * c:KYC * c + KYC]
                i = slot(j)[:, BANK * bh:BANK * (bh + 1)].rearrange("p (b y o) -> p b y o", b=BL, y=KYC)
                pairs.append((o, i))
            return pairs

        def if2_pairs(j):
            g = j - G_IF2
            o = RA[:, :].rearrange("p (t h r k) -> p t k r h", t=BH, h=H, r=2)[:, g // 4, 8 * (g % 4):8 * (g % 4) + 8]
            return [(o, slot(j).rearrange("p (k r h) -> p k r h", k=8, r=2))]

        def t3_pairs(j):
            g = j - G_T3
            return [(RB[:, 1024 * g:1024 * g + 1024], slot(j))]

        def tb_pairs(j):
            g = j - G_TB
            i = slot(j).rearrange("p (o i v j) -> p i o v j", i=Q, v=HO, j=Q)
            return [(XH[:, :, k, g // 4, 4 * (g % 4):4 * (g % 4) + 4, :].rearrange("p j o v -> p o v j"), i[:, k])
                    for k in range(Q)]

        def lt_pair(l, j):
            g = j - G_LT[l]
            if l == 0:
                return L[0][:, 1024 * g:1024 * g + 1024], slot(j)
            return by_position(L[1])[:, g], slot(j).rearrange("p (j o v) -> p j o v", j=Q, o=HO)

        CW = (E, L2)

        def centred_block(bh, t):
            return blk(RA, (2 * (t // 8) + bh) * 8 + t % 8)

        def sweep_row(s, q, u):
            if s % 2:
                q, u = HO - 1 - q, Q - 1 - u
            qs = bass.ds(q, 1)
            if s < 2:
                return XW[:, u, :, qs, :].rearrange("p b o v -> p b (o v)")
            return XV[:, u, :, :, qs].rearrange("p b o v -> p b (o v)")

        block = ctx.enter_context(nc.Block())

        @block.sync
        def _(sp):
            for g in range(4):
                sp.dma_start(RA[:, 2048 * g:2048 * g + 2048], x_in[:, 2048 * g:2048 * g + 2048]).then_inc(s_x[g], 16)
            for c in range(2):
                sp.dma_start(RE[:, WCOLS * c:WCOLS * (c + 1)], wspec[c]).then_inc(s_wc[c], 16)
            for o, i in ((conv_sb, conv_w), (convb_sb, conv_b), (gate_sb, gate_w), (gateb_sb, gate_b),
                         (w2_sb, w2), (b2_sb, b2), (own_sb, own)):
                sp.dma_start(o[:], i).then_inc(s_par, 16)
            sp.dma_start(w1_sb[:], w1[0]).then_inc(s_w1[0], 16)
            for c in range(2, NCH):
                if c == 2:
                    sp.wait_ge(s_sum, 4)
                else:
                    sp.wait_ge(s_mix, 4 * (c - 2))
                sp.dma_start(RE[:, WCOLS * (c % 3):WCOLS * (c % 3 + 1)], wspec[c]).then_inc(s_wc[c % 3], 16)
            sp.wait_ge(s_t0, NCH)
            sp.wait_ge(s_t1, NCH)
            sp.dma_start(RC, x_in).then_inc(s_xr, 16)
            sp.wait_ge(s_h, 1)
            sp.dma_start(w1_sb[:], w1[1]).then_inc(s_w1[1], 16)
            for bh in range(BH):
                wait_drained(sp, G_TB + 4 * bh + 3)
                for j in range(Q):
                    for bl in range(BL):
                        sp.dma_start(XW[C * j:C * j + C, :, BH * bl + bh],
                                     XH[C * bl:C * bl + C, j, :, bh]).then_inc(s_pw[bh], 16)
            for n in range(4):
                sp.wait_ge(s_arc, 63 + 16 * n + 15)
                o0 = HO - 4 * (n + 1)
                for j in range(Q):
                    for i in range(Q):
                        sp.dma_start(XV[C * i:C * i + C, j, :, o0:o0 + 4, :],
                                     XW[C * j:C * j + C, i, :, o0:o0 + 4, :]).then_inc(s_ph, 16)
            sp.wait_ge(s_arc, 4 * 63)
            for i in range(Q):
                for bl in range(BL):
                    sp.dma_start(CO[C * bl:C * bl + C, i], XV[C * i:C * i + C, :, BH * bl:BH * bl + BH]
                                 ).then_inc(s_co[i], 16)
            for i in range(Q):
                sp.wait_ge(s_ad, 16 + 4 * (i + 1))
                sp.dma_start(out[:, 2048 * i:2048 * i + 2048], RB[:, 2048 * i:2048 * i + 2048]).then_inc(s_out, 16)
            sp.wait_ge(s_out, 16 * Q)

        @block.gpsimd
        def _(pool):
            pool.wait_ge(s_full, G_F1 + 8)
            pool.memset(RB[:, :], 0.0).then_inc(s_zero, 1)

        @block.tensor
        def _(pe):
            def group(j, ins, rhs):
                for n, lhs in enumerate(ins):
                    if rhs is None:
                        m = pe.transpose(blk(slot(j), n), lhs, ident)
                    else:
                        m = pe.matmul(blk(slot(j), n), lhs, rhs, start=True, stop=True)
                m.then_inc(s_full, 1)

            def centre_tokens(ln, src):
                for g in range(4):
                    if g >= 2:
                        pe.wait_ge(s_nrm, 4 * ln + g - 1)
                    if ln == 0:
                        pe.wait_ge(s_x[g], 16)
                    for n in range(16):
                        m = pe.matmul(blk(banks(4 * (g % 2), 4), n), blk(src, 16 * g + n), centre,
                                      start=True, stop=True)
                    m.then_inc(s_cen, 1)

            pe.wait_ge(s_dft, 16)
            centre_tokens(0, RA)

            for g in range(8):
                pe.wait_ge(s_nrm, max(g // 2 + 1, 3 if g < 2 else 4))
                if g >= 4:
                    wait_one_drained(pe, G_F1 + g - 4)
                group(G_F1 + g, [blk(RB, 8 * g + n) for n in range(8)], fwd_w)
            for g in range(8):
                wait_drained(pe, G_F1 + (3 if g < 4 else 7))
                wait_one_drained(pe, G_T1 + g - 4)
                group(G_T1 + g, [blk(RC, 8 * g + n) for n in range(8)], None)

            def spectrum(c):
                if c == 0:
                    wait_drained(pe, G_T1 + 7)
                if c >= 2:
                    pe.wait_ge(s_xbd, c - 1)
                    pe.wait_ge(s_xba, c - 1)
                for bh in range(BH):
                    for y in range(KYC):
                        m = pe.matmul(blk(PS[:, 2 * (c % 2) + bh, :], y), blk(RA, bh * KY + c * KYC + y), fwd_h,
                                      start=True, stop=True)
                m.then_inc(s_f2, 1)

            def mix(c):
                pe.wait_ge(s_xbd, c + 1)
                pe.wait_ge(s_xba, c + 1)
                pe.wait_ge(s_wc[c % 3], 16 * (c // 3 + 1))
                for k in range(4):
                    if c >= 1:
                        pe.wait_ge(s_md if k < 2 else s_ma, 2 * (c - 1) + k % 2 + 1)
                    for n in range(8):
                        x, y = divmod(8 * k + n, KYC)
                        for a in range(2):
                            o = PS[64 * a:64 * a + 64, 4 + k, :].rearrange("p (x w y o) -> p x y w o", x=2, w=2, y=KYC)
                            m = pe.matmul(o[:, x % 2, y],
                                          XB[:, c % 2, x, 2 * y + a].rearrange("p r q b -> p (r q b)"),
                                          WR[:, c % 3, a, x, y, :], start=True, stop=True)
                    m.then_inc(s_mix, 1)

            spectrum(0)
            for c in range(NCH):
                if c + 1 < NCH:
                    spectrum(c + 1)
                mix(c)

            for c in range(NCH):
                if c == 0:
                    pe.wait_ge(s_xbd, NCH)
                    pe.wait_ge(s_xba, NCH)
                pe.wait_ge(s_md, 2 * NCH if c else 2)
                pe.wait_ge(s_ma, 2 * NCH if c else 2)
                if c >= 2:
                    pe.wait_ge(s_comb, c - 1)
                    pe.wait_ge(s_tmp, c - 1)
                for w, s in ((0, s_t0), (1, s_t1)):
                    for x in range(X8):
                        m = pe.transpose(blk(banks(4 * (c % 2) + 2 * w, 2), x), Z[:, c, x, w], ident)
                    m.then_inc(s, 1)
            pe.wait_ge(s_comb, NCH)
            pe.wait_ge(s_tmp, NCH)
            for c in range(NCH):
                if c >= 4:
                    wait_one_drained(pe, G_T2 + c - 4)
                group(G_T2 + c, [V_of_b[:, c, :, b] for b in range(B)], None)
            for g in range(8):
                wait_drained(pe, G_T2 + 2 * (g % 4) + 1)
                wait_one_drained(pe, G_IF2 + g - 4)
                group(G_IF2 + g, [blk(RB, 8 * g + n) for n in range(8)], inv_h)
            for g in range(8):
                wait_drained(pe, G_IF2 + (3 if g < 4 else 7))
                wait_one_drained(pe, G_T3 + g - 4)
                group(G_T3 + g, [blk(RA, 8 * g + n) for n in range(8)], None)
            for g in range(8):
                wait_drained(pe, G_T3 + min(g + 4, 7))
                if g >= 4:
                    pe.wait_ge(s_res, g - 3)
                for n in range(8):
                    m = pe.matmul(blk(banks(2 * (g % 4), 2), n), blk(RB, 8 * g + n), inv_w, start=True, stop=True)
                m.then_inc(s_if1, 1)

            pe.wait_ge(s_res, 8)
            pe.wait_ge(s_par, 16 * N_PAR)
            for l in range(2):
                m = pe.matmul(PS[:, l, 0:BL * NE], centre, gate_sb[:, l, :], start=True, stop=True)
            m.then_inc(s_gp, 1)

            def experts(l):
                pe.wait_ge(s_gpc, 3)
                for g in range(8):
                    if l == 1:
                        pe.wait_ge(s_x3, 2 * (g // 2) + 2)
                    if g >= 2:
                        pe.wait_ge(s_lg, 8 * l + g - 1)
                    for n in range(8):
                        t, bh = 8 * (g // 2) + n, g % 2
                        src = blk(RC, bh * NT + t) if l == 0 else blk(RB, (2 * (t // 2) + bh) * 2 + t % 2)
                        m = pe.matmul(PS[:, 4 * (g % 2) + n // 2, 192 * (n % 2):192 * (n % 2) + 192], src,
                                      proj[:, l, :], start=True, stop=True)
                    m.then_inc(s_pr, 1)
                pe.wait_ge(s_lg, 8 * l + 8)
                for g in range(4):
                    group(G_LT[l] + g, [LT[:, 8 * g + n].rearrange("p h n -> p (h n)") for n in range(8)], None)
                wait_drained(pe, G_LT[l] + 3)
                pe.wait_ge(s_rs, l + 1)
                pe.transpose(PS[0:1, 6, 0:P], rsum[:, :], ident).then_inc(s_rt, 1)

                def pool_tokens(g):
                    pe.wait_ge(s_wtd, 4 * l + g + 1)
                    for t in range(8 * g, 8 * g + 8):
                        for bh in range(BH):
                            m = pe.matmul(PS[:, 4 + bh, 0:P], centred_block(bh, t), WTOK[:, t, :],
                                          start=(t == 0), stop=(t == NT - 1))
                    return m

                for g in range(4):
                    pe.wait_ge(s_ord if l else s_msk, g + 1)
                    if g >= 2:
                        pe.wait_ge(s_wtd, 4 * l + g - 1)
                    for n in range(8):
                        m = pe.transpose(blk(banks(2 * (g % 2), 2), n), blk(CW[l], 8 * g + n), ident)
                    m.then_inc(s_wt, 1)
                    if g == 1:
                        pe.wait_ge(s_rr, l + 1)
                        pe.matmul(PS[0:C, 7, 0:P], ones[:, :], rs_row[:, :], start=True, stop=True).then_inc(s_rb, 1)
                    if g >= 1:
                        pool_tokens(g - 1)
                pool_tokens(3).then_inc(s_pl, 1)
                pe.wait_ge(s_pc, l + 1)
                pe.wait_ge(s_w1[l], 16)
                for e in range(NE):
                    m = pe.matmul(PS[:, 6, B * e:B * e + B], w1_sb[:, e, :], pooled[:, :, e], start=True, stop=True)
                m.then_inc(s_h, 1)
                pe.wait_ge(s_g, l + 1)
                for e in range(NE):
                    m = pe.matmul(PS[0:C, 7, B * e:B * e + B], w2_sb[:, l, e, :], hid[:, e, :], start=True, stop=True)
                m.then_inc(s_o, 1)
                pe.wait_ge(s_ob, l + 1)
                pe.transpose(PS[:, 4, 0:C], eout[:, :, :].rearrange("p b e -> p (b e)"),
                             ident[0:C, 0:C]).then_inc(s_ot, 1)
                pe.wait_ge(s_os, l + 1)
                for k in range(16):
                    if k >= 4:
                        pe.wait_ge(s_ad, 16 * l + k - 3)
                    if l == 0:
                        bh, ch = divmod(k, 8)
                    else:
                        ch, bh = divmod(k, 2)
                    rhs = CW[l][:, ch * BANK:(ch + 1) * BANK]
                    pe.matmul(PS[:, k % 4, :], espread[:, BL * bh:BL * bh + BL, :].rearrange("p b o -> p (b o)"), rhs,
                              start=True, stop=True).then_inc(s_sc, 1)

            experts(0)

            pe.wait_ge(s_ad, 16)
            centre_tokens(1, RC)
            for g in range(8):
                pe.wait_ge(s_nrm, 4 + max(g // 2 + 1, 3 if g < 2 else 4))
                if g >= 4:
                    wait_one_drained(pe, G_TB + g - 4)
                group(G_TB + g, [blk(RA, 8 * g + n) for n in range(8)], None)

            wait_drained(pe, G_TB + 7)
            for s in range(4):
                def step(q, u):
                    pe.wait_ge(s_st, 64 * s + Q * q + u)
                    for d in range(3):
                        m = pe.matmul(PS[:, u % 2, 0:P].rearrange("p (b v) -> p b v", b=B), conv_sb[:, s, d, :],
                                      state[:, (u + 1) % 2, :, d:d + HO], start=(d == 0), stop=(d == 2))
                    m.then_inc(s_cv, 1)
                    for _ in range(4):
                        pe.matmul(PS[:, 2, 0:P], warm[:, :], warm[:, :], start=True, stop=True)

                for u in range(1, Q):
                    step(0, u)
                with pe.Fori(1, HO) as q:
                    for u in range(Q):
                        step(q, u)

            experts(1)

        @block.scalar
        def _(act):
            act.dma_start(dft_sb[:], dft).then_inc(s_dft, 16)

            def root(n, first, width, eps):
                act.wait_ge(s_sum, n + 1)
                act.activation(std[:, first:first + width], sums[:, first:first + width], ACT.Sqrt, bias=eps,
                               scale=1.0 / C).then_inc(s_std, 1)

            def norm_tokens(ln):
                for g in range(4):
                    act.wait_ge(s_cen, 4 * ln + g + 1)
                    if LN0[ln] + g >= 2:
                        act.wait_ge(s_sum, LN0[ln] + g - 1)
                    act.activation(square[:, g % 2, :], banks(4 * (g % 2), 4), ACT.Square).then_inc(s_sq, 1)
                    if g >= 1:
                        root(LN0[ln] + g - 1, 64 * (g - 1), 64, eps_sb[:, 0:1])
                root(LN0[ln] + 3, 192, 64, eps_sb[:, 0:1])

            def drain(j, pairs):
                act.wait_ge(s_full, j + 1)
                for o, i in pairs(j):
                    m = act.copy(o, i)
                m.then_inc(s_da, 1)

            act.wait_ge(s_set, N_SET)
            norm_tokens(0)
            for j in range(G_F1, G_F1 + 8, 2):
                drain(j, f1_pairs)
            for j in range(G_T1, G_T1 + 8, 2):
                drain(j, t1_pairs)

            def spread(c):
                act.wait_ge(s_f2, c + 1)
                if c == 0:
                    act.wait_ge(s_zero, 1)
                if c >= 2:
                    act.wait_ge(s_mix, 4 * (c - 1))
                for o, i in xb_pairs(c, 1):
                    m = act.copy(o, i)
                m.then_inc(s_xba, 1)

            spread(0)
            for c in range(NCH):
                if c + 1 < NCH:
                    spread(c + 1)
                for k in (2, 3):
                    act.wait_ge(s_mix, 4 * c + k + 1)
                    act.copy(z_bank(c, k), PS[:, 4 + k, :]).then_inc(s_ma, 1)
            for c in range(NCH):
                act.wait_ge(s_t1, c + 1)
                if c >= 2:
                    act.wait_ge(s_comb, c - 1)
                act.copy(imtmp[:, c % 2, :], banks(4 * (c % 2) + 2, 2)).then_inc(s_tmp, 1)
            for j in range(G_T2, G_T2 + 8, 2):
                drain(j, t2_pairs)
            for j in range(G_IF2, G_IF2 + 8, 2):
                drain(j, if2_pairs)
            for j in range(G_T3, G_T3 + 8, 2):
                drain(j, t3_pairs)

            def experts(l):
                for g in range(8):
                    act.wait_ge(s_pr, 8 * l + g + 1)
                    xc = PS[:, 4 * (g % 2):4 * (g % 2) + 4, 0:384].rearrange("p k (j n) -> p k j n", j=2)[:, :, :, 0:P]
                    act.copy(RA[:, 1024 * g:1024 * g + 1024].rearrange("p (k j n) -> p k j n", k=4, j=2),
                             xc).then_inc(s_xc, 1)
                    act.wait_ge(s_sum, EX0[l] + g - 1)
                    act.activation(square[:, g % 2, 0:1024].rearrange("p (k j n) -> p k j n", k=4, j=2), xc,
                                   ACT.Square).then_inc(s_sq, 1)
                    if g >= 1:
                        root(EX0[l] + g - 1, 32 * (g - 1), 32, eps_sb[:, 1:2])
                root(EX0[l] + 7, 224, 32, eps_sb[:, 1:2])
                for j in (G_LT[l], G_LT[l] + 2):
                    act.wait_ge(s_full, j + 1)
                    o, i = lt_pair(l, j)
                    act.activation(o, i, ACT.Identity, bias=gateb_sb[:, l:l + 1]).then_inc(s_da, 1)
                act.wait_ge(s_nm, l + 1)
                act.activation(E, L[l], ACT.Exp, bias=negmax[:, :], accum_out=expsum[:, :]).then_inc(s_exp, 1)
                if l == 1:
                    for i in range(Q):
                        act.wait_ge(s_msk, 8)
                        act.copy(CW[1][:, 1024 * i:1024 * i + 1024].rearrange("p (j o v) -> p j o v", j=Q, o=HO),
                                 by_position(E)[:, i]).then_inc(s_ord, 1)
                act.wait_ge(s_rt, l + 1)
                act.copy(rs_row[:, :], PS[0:1, 6, 0:P]).then_inc(s_rr, 1)
                act.wait_ge(s_rb, l + 1)
                act.copy(rs_rep[:, :], PS[0:C, 7, 0:P]).then_inc(s_rp, 1)
                act.wait_ge(s_h, l + 1)
                act.activation(hid[:, :, :].rearrange("p e b -> p (e b)"), PS[:, 6, 0:P], ACT.Gelu).then_inc(s_g, 1)

            act.wait_ge(s_par, 16 * N_PAR)
            experts(0)

            norm_tokens(1)
            for j in range(G_TB, G_TB + 8, 2):
                drain(j, tb_pairs)

            for s in range(4):
                if s == 0:
                    for bh in range(BH):
                        act.wait_ge(s_pw[bh], 16 * Q * BL)
                elif s == 2:
                    act.wait_ge(s_ph, 16 * 4 * Q * Q)
                else:
                    act.wait_ge(s_arc, 63 * s)

                def fetch(q, u):
                    act.activation(rowb[:, u], sweep_row(s, q, u), ACT.Identity,
                                   bias=convb_sb[:, s:s + 1]).then_inc(s_row, 1)

                def archive(q, u):
                    act.wait_ge(s_st, 64 * s + Q * q + u + 1)
                    act.copy(sweep_row(s, q, u), state[:, u % 2, :, 1:1 + HO]).then_inc(s_arc, 1)

                if s:
                    act.wait_ge(s_st, 64 * s)
                for t in range(1, 5):
                    fetch(t // Q, t % Q)
                for u in range(1, Q):
                    archive(0, u)
                    fetch(1, u)
                with act.Fori(1, HO - 1) as q:
                    for u in range(Q):
                        archive(q, u)
                        fetch(q + 1, u)
                for u in range(Q):
                    archive(HO - 1, u)

            experts(1)

        @block.vector
        def _(dve):
            dve.memset(eps_sb[:, 0:1], LN_C_EPS[0]).then_inc(s_set, 1)
            dve.memset(eps_sb[:, 1:2], LN_T_EPS).then_inc(s_set, 1)
            dve.memset(state[:, :, :, :], 0.0).then_inc(s_set, 1)
            dve.memset(ones[:, :], 1.0).then_inc(s_set, 1)
            dve.memset(pooled[C:C + 1, :, :], 1.0).then_inc(s_set, 1)
            dve.memset(warm[:, :], 0.0).then_inc(s_set, 1)

            def norm_tokens(ln, dst):
                def total(g):
                    dve.wait_ge(s_sq, LN0[ln] + g + 1)
                    dve.tensor_reduce(sums[:, 64 * g:64 * g + 64],
                                      square[:, g % 2, :].rearrange("p (a c) -> p a c", c=C), AX_X,
                                      ALU.add).then_inc(s_sum, 1)

                total(0)
                for g in range(4):
                    if g < 3:
                        total(g + 1)
                    dve.wait_ge(s_std, LN0[ln] + g + 1)
                    dve.reciprocal(rstd[:, 64 * g:64 * g + 64], std[:, 64 * g:64 * g + 64]).then_inc(s_rec, 1)
                    dve.wait_ge(s_rec, LN0[ln] + g + 1)
                    dve.tensor_tensor(dst[:, 2048 * g:2048 * g + 2048].rearrange("p (a c) -> p a c", c=C),
                                      banks(4 * (g % 2), 4).rearrange("p (a c) -> p a c", c=C),
                                      rstd[:, 64 * g:64 * g + 64].unsqueeze(2).to_broadcast([P, 64, C]),
                                      ALU.mult).then_inc(s_nrm, 1)

            def drain(j, pairs):
                dve.wait_ge(s_full, j + 1)
                for o, i in pairs(j):
                    m = dve.tensor_copy(o, i)
                m.then_inc(s_dd, 1)

            norm_tokens(0, RB)
            for j in range(G_F1 + 1, G_F1 + 8, 2):
                drain(j, f1_pairs)
            for j in range(G_T1 + 1, G_T1 + 8, 2):
                drain(j, t1_pairs)

            def spread(c):
                dve.wait_ge(s_f2, c + 1)
                if c == 0:
                    dve.wait_ge(s_zero, 1)
                if c >= 2:
                    dve.wait_ge(s_mix, 4 * (c - 1))
                for o, i in xb_pairs(c, 0):
                    m = dve.tensor_copy(o, i)
                m.then_inc(s_xbd, 1)

            spread(0)
            for c in range(NCH):
                if c + 1 < NCH:
                    spread(c + 1)
                for k in (0, 1):
                    dve.wait_ge(s_mix, 4 * c + k + 1)
                    dve.tensor_copy(z_bank(c, k), PS[:, 4 + k, :]).then_inc(s_md, 1)
            for c in range(NCH):
                dve.wait_ge(s_t0, c + 1)
                dve.wait_ge(s_tmp, c + 1)
                by_re = banks(4 * (c % 2), 2).rearrange("p (x a r n) -> p x a r n", x=X8, a=2, r=2)
                by_im = imtmp[:, c % 2, :].rearrange("p (x a r n) -> p x a r n", x=X8, a=2, r=2)
                dve.tensor_tensor(V[:, c, :, :, 0, :], by_re[:, :, :, 0, :], by_im[:, :, :, 1, :], ALU.subtract)
                dve.tensor_tensor(V[:, c, :, :, 1, :], by_re[:, :, :, 1, :], by_im[:, :, :, 0, :],
                                  ALU.add).then_inc(s_comb, 1)
            for j in range(G_T2 + 1, G_T2 + 8, 2):
                drain(j, t2_pairs)
            for j in range(G_IF2 + 1, G_IF2 + 8, 2):
                drain(j, if2_pairs)
            for j in range(G_T3 + 1, G_T3 + 8, 2):
                drain(j, t3_pairs)
            dve.wait_ge(s_xr, 16)
            for g in range(8):
                dve.wait_ge(s_if1, g + 1)
                x1 = RC[:, 1024 * g:1024 * g + 1024]
                dve.tensor_tensor(x1, banks(2 * (g % 4), 2), x1, ALU.add).then_inc(s_res, 1)

            dve.wait_ge(s_par, 16 * N_PAR)
            dve.tensor_scalar(negb_sb[:, :], convb_sb[:, :], -1.0, None, ALU.mult).then_inc(s_gpc, 1)
            dve.tensor_copy(proj[:, :, 0:P], centre.unsqueeze(1).to_broadcast([P, 2, P])).then_inc(s_gpc, 1)
            dve.wait_ge(s_gp, 1)
            dve.tensor_copy(proj[:, :, P:], PS[:, 0:2, 0:BL * NE]).then_inc(s_gpc, 1)

            def experts(l):
                def total(g):
                    dve.wait_ge(s_sq, EX0[l] + g + 1)
                    dve.tensor_reduce(sums[:, 32 * g:32 * g + 32],
                                      square[:, g % 2, 0:1024].rearrange("p (a c) -> p a c", c=C), AX_X,
                                      ALU.add).then_inc(s_sum, 1)

                def scale(g):
                    t0, bh = 8 * (g // 2), g % 2
                    r = rstd[:, :].rearrange("p (t h b) -> p h t b", h=BH, b=BL)[:, bh, t0:t0 + 8, :]
                    dve.wait_ge(s_std, EX0[l] + g + 1)
                    dve.reciprocal(r, std[:, 32 * g:32 * g + 32].rearrange("p (t b) -> p t b", b=BL)
                                   ).then_inc(s_rec, 1)
                    dve.wait_ge(s_rec, EX0[l] + g + 1)
                    for n in range(2):
                        raw = PS[:, 4 * (g % 2):4 * (g % 2) + 4, 192 * n + P:192 * n + 192]
                        m = dve.tensor_tensor(
                            LT[:, t0 + n:t0 + 8:2, bh, :].rearrange("p t (b e) -> p t b e", e=NE),
                            raw.rearrange("p t (b e) -> p t b e", e=NE),
                            r[:, n::2, :].unsqueeze(3).to_broadcast([P, 4, BL, NE]), ALU.mult)
                    m.then_inc(s_lg, 1)

                total(0)
                for g in range(8):
                    if g < 7:
                        total(g + 1)
                    scale(g)
                for j in (G_LT[l] + 1, G_LT[l] + 3):
                    dve.wait_ge(s_full, j + 1)
                    o, i = lt_pair(l, j)
                    dve.tensor_scalar(o, i, gateb_sb[:, l:l + 1], None, ALU.add).then_inc(s_dd, 1)
                wait_drained(dve, G_LT[l] + 3)
                dve.max(top8[:, :], L[l]).then_inc(s_mx, 1)
                dve.wait_ge(s_mx, l + 1)
                dve.tensor_scalar(negmax[:, :], top8[:, 0:1], -1.0, None, ALU.mult).then_inc(s_nm, 1)
                dve.match_replace(L2, top8[:, :], L[l], MASKED).then_inc(s_rep, 1)
                dve.wait_ge(s_exp, l + 1)
                dve.reciprocal(rsum[:, :], expsum[:, :]).then_inc(s_rs, 1)
                dve.wait_ge(s_rep, l + 1)
                for g in range(4):
                    c = slice(1024 * g, 1024 * g + 1024)
                    dve.scalar_tensor_tensor(out=E[:, c], in0=L2[:, c], scalar=MASKED / 2, in1=E[:, c],
                                             op0=ALU.is_le, op1=ALU.mult).then_inc(s_msk, 1)
                for g in range(4):
                    dve.wait_ge(s_wt, 4 * l + g + 1)
                    dve.tensor_tensor(WTOK[:, 8 * g:8 * g + 8, :].rearrange("p t (b e) -> p (t b) e", e=NE),
                                      banks(2 * (g % 2), 2).rearrange("p (a e) -> p a e", e=NE),
                                      rstd[:, 64 * g:64 * g + 64].unsqueeze(2).to_broadcast([P, 64, NE]),
                                      ALU.mult).then_inc(s_wtd, 1)
                dve.wait_ge(s_pl, l + 1)
                dve.wait_ge(s_rp, l + 1)
                for b in range(B):
                    bh, bl = divmod(b, BL)
                    m = dve.tensor_tensor(pooled[0:C, b, :], PS[C * bl:C * bl + C, 4 + bh, NE * b:NE * b + NE],
                                          rs_rep[:, NE * b:NE * b + NE], ALU.mult)
                m.then_inc(s_pc, 1)
                dve.wait_ge(s_o, l + 1)
                dve.tensor_tensor(eout[:, :, :].rearrange("p b e -> p e b"),
                                  PS[0:C, 7, 0:P].rearrange("p (e b) -> p e b", b=B),
                                  b2_sb[:, l, :].unsqueeze(2).to_broadcast([C, NE, B]), ALU.add).then_inc(s_ob, 1)
                dve.wait_ge(s_ot, l + 1)
                dve.scalar_tensor_tensor(out=espread[:, :, :],
                                         in0=PS[:, 4, 0:C].unsqueeze(1).to_broadcast([P, B, C]),
                                         scalar=rsum[:, :], in1=own_sb[:, :].unsqueeze(2).to_broadcast([P, B, C]),
                                         op0=ALU.mult, op1=ALU.mult).then_inc(s_os, 1)
                for k in range(16):
                    dve.wait_ge(s_sc, 16 * l + k + 1)
                    if l == 0:
                        x2 = RC[:, BANK * k:BANK * (k + 1)]
                        dve.tensor_tensor(x2, PS[:, k % 4, :], x2, ALU.add).then_inc(s_ad, 1)
                    else:
                        i, j, bh = k // 4, k // 2 % 2 * 2, k % 2
                        x4 = X3[:, i, j:j + 2, bh].rearrange("p j o v -> p j (o v)")
                        dve.tensor_tensor(x4, PS[:, k % 4, :].rearrange("p (j n) -> p j n", j=2), x4,
                                          ALU.add).then_inc(s_ad, 1)

            experts(0)

            norm_tokens(1, RA)
            for j in range(G_TB + 1, G_TB + 8, 2):
                drain(j, tb_pairs)

            for s in range(4):
                if s == 0:
                    for bh in range(BH):
                        dve.wait_ge(s_pw[bh], 16 * Q * BL)
                elif s == 2:
                    dve.wait_ge(s_ph, 16 * 4 * Q * Q)
                else:
                    dve.wait_ge(s_arc, 63 * s)
                dve.tensor_copy(state[:, 0, :, 1:1 + HO], sweep_row(s, 0, 0)).then_inc(s_st, 1)

                def step(q, u):
                    t = Q * q + u
                    dve.wait_ge(s_row, 63 * s + t)
                    if not isinstance(q, int) or t >= 3:
                        dve.wait_ge(s_arc, 63 * s + t - 2)
                    dve.wait_ge(s_cv, 63 * s + t)
                    dve.scalar_tensor_tensor(out=state[:, u % 2, :, 1:1 + HO],
                                             in0=PS[:, u % 2, 0:P].rearrange("p (b v) -> p b v", b=B),
                                             scalar=negb_sb[:, s:s + 1], in1=rowb[:, u],
                                             op0=ALU.max, op1=ALU.add).then_inc(s_st, 1)

                for u in range(1, Q):
                    step(0, u)
                with dve.Fori(1, HO) as q:
                    for u in range(Q):
                        step(q, u)

            for k in range(8):
                i, bh = divmod(k, 2)
                dve.wait_ge(s_co[i], 16 * BL)
                dve.tensor_tensor(X3[:, i, :, bh], CO[:, i, :, bh],
                                  by_position(RC[:, TOK * bh:TOK * (bh + 1)])[:, i], ALU.add).then_inc(s_x3, 1)

            experts(1)


def dft_tables():
    f = np.float64
    centre = np.eye(P, dtype=f) - np.kron(np.eye(BL), np.full((C, C), 1.0 / C))
    w, ky = np.arange(W), np.arange(KY)
    a = 2 * np.pi * np.outer(w, ky) / W
    fwd_w = np.kron(np.eye(2), np.concatenate([np.cos(a), -np.sin(a)], 1) / W)
    h, kx = np.arange(H), np.arange(H)
    a = 2 * np.pi * np.outer(h, kx) / H
    c, s = np.cos(a), np.sin(a)
    full = np.array([[c, -s], [s, c]]) / H
    fwd_h = full.transpose(0, 2, 3, 1).reshape(2, H, 2, Q, X8, 2)
    fwd_h = fwd_h.transpose(0, 1, 2, 3, 5, 4).reshape(P, P)
    inv = np.array([[c, s], [-s, c]])
    inv_h = inv.transpose(3, 0, 1, 2).reshape(2, Q, X8, 2, 2, H)
    inv_h = inv_h.transpose(2, 0, 3, 1, 4, 5).reshape(P, P)
    a = 2 * np.pi * np.outer(ky, w) / W
    twice = np.where(ky == 0, 1.0, 2.0)[:, None]
    inv_w = np.kron(np.eye(2), np.concatenate([twice * np.cos(a), -twice * np.sin(a)], 0))
    return np.ascontiguousarray(np.stack([centre, np.eye(P), fwd_w, fwd_h, inv_h, inv_w], 1).astype(np.float32))


def banded(w):
    m = np.zeros((Q, C, 3, Q, C), w.dtype)
    for d in range(3):
        for i in range(Q):
            for j in range(Q):
                k = Q * (d - 1) + i - j + TAPS // 2
                if 0 <= k < TAPS:
                    m[i, :, d, j, :] = w[:, :, k].T
    return m.reshape(P, 3, P)


def kernel(**inputs):
    import concourse.bacc as bacc
    from concourse.bass_utils import run_bass_kernel_spmd

    a = {k: np.asarray(v) for k, v in inputs.items()}
    x = a["x"].reshape(BH, BL, C, TOK).transpose(1, 2, 0, 3).reshape(P, NF)
    ws = np.stack([np.stack([a[f"L0_conv_w{n}_{p}"] for p in ("real", "imag")]) for n in (1, 2)])
    ws = ws.reshape(2, 2, C, C, Q, X8, NCH, KYC).transpose(6, 4, 2, 0, 5, 7, 1, 3).reshape(NCH, P, WCOLS)
    conv_w = np.stack([banded(a[f"L1_conv_w_{s}"]) for s in "durl"], 1)
    conv_b = np.stack([np.tile(a[f"L1_conv_b_{s}"], Q) for s in "durl"], 1)
    gate = np.zeros((BL, C, 2, BL, NE), np.float32)
    for l in range(2):
        for b in range(BL):
            gate[b, :, l, b, :] = a[f"L{l}_ffn_gate_w"].T
    gate_b = np.stack([np.tile(a[f"L{l}_ffn_gate_b"], B) for l in range(2)], 1)
    w1 = np.stack([a[f"L{l}_ffn_weight1"].transpose(1, 0, 2) for l in range(2)])
    w2 = np.stack([a[f"L{l}_ffn_weight2"][:, :NHID].transpose(1, 0, 2) for l in range(2)], 1)
    b2 = np.stack([a[f"L{l}_ffn_weight2"][:, NHID].T for l in range(2)], 1)
    own = np.repeat(np.eye(B, dtype=np.float32), NE, 0)
    arrays = {"x_in": x, "dft": dft_tables(), "wspec": ws, "conv_w": conv_w, "conv_b": conv_b,
              "gate_w": gate.reshape(P, 2, BL * NE), "gate_b": gate_b, "w1": w1, "w2": w2, "b2": b2, "own": own}
    arrays = {k: np.ascontiguousarray(v) for k, v in arrays.items()}

    nc = bacc.Bacc("TRN2", target_bir_lowering=False, num_devices=1)
    args = [nc.dram_tensor(k, v.shape, F32, kind="ExternalInput").ap() for k, v in arrays.items()]
    args.append(nc.dram_tensor("out", (P, NF), F32, kind="ExternalOutput").ap())
    build_kernel(nc, *args)
    r = run_bass_kernel_spmd(nc, [arrays], core_ids=[0])
    y = np.asarray(r.results[0]["out"])
    y = y.reshape(BL, C, Q, Q, BH, HO, HO).transpose(4, 0, 1, 5, 2, 6, 3)
    return np.ascontiguousarray(y.reshape(B, C, H, W))
```

```python
from contextlib import ExitStack

import numpy as np

import concourse.bass as bass
from concourse import mybir

B, C, H, W = 8, 32, 64, 64
P = 128
BL, BH = P // C, B * C // P
TOK = H * W
KY = W // 2
NE, NHID = 16, 128
Q = 4
HO = H // Q
TAPS = 9
NT = TOK // P
BANK = 512
KYC = 4
NCH = KY // KYC
X8 = H // 2 // Q
WCOLS = 2 * X8 * KYC * 2 * C
NF = BH * TOK
LN_C_EPS, LN_T_EPS = (1e-6, 1e-6), 1e-5
MASKED = -3.0e38

F32 = mybir.dt.float32
BF16 = mybir.dt.bfloat16
ALU = mybir.AluOpType
ACT = mybir.ActivationFunctionType
AX_X = mybir.AxisListType.X


def build_kernel(nc, x_in, dft, wspec, conv_w, conv_b, gate_w, gate_b, w1, w2, b2, own, out):
    with ExitStack() as ctx:
        def sb(name, shape, dt=F32):
            return ctx.enter_context(nc.sbuf_tensor(name, shape, dt))

        def sem(name):
            return ctx.enter_context(nc.semaphore(name))

        RA, RB, RCD = sb("RA", [P, NF]), sb("RB", [P, NF]), sb("RCD", [P, 2 * NF])
        RC, RD = RCD[:, 0:NF], RCD[:, NF:2 * NF]
        RE = sb("RE", [P, 3 * WCOLS])
        PS = ctx.enter_context(nc.psum_tensor("PS", [P, 8, BANK], F32))

        dft_sb = sb("dft_sb", [P, 6, P])
        centre, ident, fwd_w, fwd_h, inv_h, inv_w = (dft_sb[:, i, :] for i in range(6))
        own_sb = sb("own_sb", [P, B])
        conv_sb = sb("conv_sb", [P, 4, 3, P])
        convb_sb, negb_sb = sb("convb_sb", [P, 4]), sb("negb_sb", [P, 4])
        gate_sb = sb("gate_sb", [P, 2, BL * NE])
        proj = sb("proj", [P, 2, P + BL * NE])
        gateb_sb = sb("gateb_sb", [P, 2])
        w1_sb = sb("w1_sb", [C + 1, NE, NHID])
        w2_sb, b2_sb = sb("w2_sb", [P, 2, NE, C]), sb("b2_sb", [C, 2, NE])
        eps_sb = sb("eps_sb", [P, 2])
        sums, std, rstd = sb("sums", [P, 256]), sb("std", [P, 256]), sb("rstd", [P, 256])
        top8 = sb("top8", [P, 8])
        negmax, expsum, rsum = sb("negmax", [P, 1]), sb("expsum", [P, 1]), sb("rsum", [P, 1])
        ones = sb("ones", [1, C])
        rs_row, rs_rep = sb("rs_row", [1, P]), sb("rs_rep", [C, P])
        pooled = sb("pooled", [C + 1, B, NE])
        hid = sb("hid", [P, NE, B])
        eout = sb("eout", [C, B, NE])
        espread = sb("espread", [P, B, C])
        state = sb("state", [P, 2, B, HO + 2])
        warm = sb("warm", [P, P], BF16)

        s_x = [sem(f"x_loaded{i}") for i in range(8)]
        s_dft, s_par = sem("dft_loaded"), sem("params_loaded")
        s_w1 = [sem(f"w1_loaded{i}") for i in range(2)]
        s_wc = [sem(f"wspec_loaded{i}") for i in range(3)]
        s_xr = sem("x_reloaded")
        s_set, s_zero = sem("memsets_done"), sem("xb_zeroed")
        s_gp, s_gpc = sem("gate_projected"), sem("gate_copied")
        s_cen, s_sq, s_sum = sem("ln_centred"), sem("squared"), sem("summed")
        s_std, s_rec, s_nrm = sem("std_ready"), sem("rstd_ready"), sem("ln_normed")
        s_full, s_da, s_dd = sem("group_full"), sem("group_drained_act"), sem("group_drained_dve")
        s_f2, s_xba, s_xbd = sem("spectrum_full"), sem("xb_written_act"), sem("xb_written_dve")
        s_mix, s_ma, s_md = sem("mixed"), sem("mix_drained_act"), sem("mix_drained_dve")
        s_t0, s_t1 = sem("products_re_turned"), sem("products_im_turned")
        s_tmp, s_comb = sem("products_im_copied"), sem("products_combined")
        s_if1, s_res = sem("image_full"), sem("residual_added")
        s_pr, s_lg = sem("projected"), sem("logits_scaled")
        s_mx, s_nm, s_rep = sem("top8_found"), sem("negmax_ready"), sem("top8_replaced")
        s_exp, s_rs, s_msk = sem("exps_ready"), sem("rsum_ready"), sem("weights_masked")
        s_ord = sem("weights_ordered")
        s_wt, s_wtd = sem("weights_turned"), sem("weights_scaled")
        s_rt, s_rr = sem("rsum_turned"), sem("rsum_row_copied")
        s_rb, s_rp = sem("rsum_spread"), sem("rsum_rep_copied")
        s_pl, s_pc = sem("pooled_full"), sem("pooled_copied")
        s_h, s_g = sem("hidden_full"), sem("gelu_done")
        s_o, s_ob = sem("experts_full"), sem("experts_biased")
        s_ot, s_os = sem("experts_turned"), sem("experts_spread")
        s_sc, s_ad = sem("scatter_full"), sem("scatter_added")
        s_ff, s_fd = sem("follower_full"), sem("follower_drained")
        s_st, s_cv = sem("state_ready"), sem("conv_ready")
        s_row, s_arc = sem("row_fetched"), sem("row_archived")
        s_ph = [sem(f"columns_in{j}") for j in range(Q)]
        s_co = [sem(f"conv_out{i}") for i in range(Q)]
        s_x3, s_out = sem("conv_added"), sem("stored")
        N_SET, N_PAR = 6, 7

        def blk(region, n):
            return region[:, n * P:(n + 1) * P]

        def banks(b0, nb):
            return PS[:, b0:b0 + nb, :].rearrange("p k c -> p (k c)")

        XB = RB[:, :].rearrange("p (s x z r q b) -> p s x z r q b", s=2, x=X8, z=2 * KYC, r=2, q=Q)
        Z = RCD[:, :].rearrange("p (c x w n) -> p c x w n", c=NCH, x=X8, w=2)
        V = RA[:, :].rearrange("p (c x a r n) -> p c x a r n", c=NCH, x=X8, a=2, r=2)
        V_of_b = RA[:, :].rearrange("p (c m b) -> p c m b", c=NCH, b=B)
        WR = RE[:, :].rearrange("p (s a x y n) -> p s a x y n", s=3, a=2, x=X8, y=KYC)
        imtmp = RE[:, 0:2 * 1024].rearrange("p (s n) -> p s n", s=2)
        square = RE[:, 2 * WCOLS:3 * WCOLS].rearrange("p (s n) -> p s n", s=2)
        LT = RD[:, 0:TOK].rearrange("p (t h n) -> p t h n", h=BH, t=NT)
        L = (RB[:, 0:TOK], RC[:, 0:TOK])
        L2, E = RD[:, 0:TOK], RD[:, TOK:2 * TOK]
        WTOK = RE[:, 0:WCOLS].rearrange("p (t n) -> p t n", t=NT)
        XW = RD.rearrange("p (i b o v) -> p i b o v", i=Q, b=B, o=HO)
        XV = RE[:, 0:NF].rearrange("p (j b o v) -> p j b o v", j=Q, b=B, o=HO)
        CO = RA[:, :].rearrange("p (i j t o v) -> p i j t o v", i=Q, j=Q, t=BH, o=HO)
        X3 = RB[:, :].rearrange("p (i j t o v) -> p i j t o v", i=Q, j=Q, t=BH, o=HO)

        rowb = RA[:, 0:4 * P].rearrange("p (s b v) -> p s b v", s=4, b=B)

        def by_position(ap):
            return ap.rearrange("p (o i v j) -> p i j o v", i=Q, v=HO, j=Q)

        G_T1, G_T2, G_IF2, G_T3 = 0, 8, 16, 24
        G_LT = (32, 36)
        LN0, EX0 = (0, 16), (8, 24)

        def slot(j):
            return banks(2 * (j % 4), 2)

        def wait_drained(eng, j):
            eng.wait_ge(s_da, j // 2 + 1)
            if j >= 1:
                eng.wait_ge(s_dd, (j + 1) // 2)

        def wait_one_drained(eng, j):
            eng.wait_ge(s_dd if j % 2 else s_da, j // 2 + 1)

        def f1_pairs(g, i):
            o = RC.rearrange("p (t k r h) -> p t h r k", t=BH, k=KY, r=2)[:, g // 4, 16 * (g % 4):16 * (g % 4) + 16]
            return [(o, i.rearrange("p (h r k) -> p h r k", r=2, k=KY))]

        def t1_pairs(j):
            g = j - G_T1
            return [(RA[:, 1024 * g:1024 * g + 1024], slot(j))]

        def xb_pairs(c, bh):
            pairs = []
            for bl in range(BL):
                for q in range(Q):
                    i = PS[C * bl:C * bl + C, 2 * (c % 2) + bh, :].rearrange("p (z q r x) -> p q z r x", q=Q, r=2, x=X8)
                    o = XB[C * q:C * q + C, c % 2, :, :, :, q, bh * BL + bl].rearrange("p x z r -> p z r x")
                    pairs.append((o, i[:, q]))
            return pairs

        def z_bank(c, k):
            return RCD[:, 2048 * c + BANK * k:2048 * c + BANK * (k + 1)]

        def t2_pairs(j):
            c = j - G_T2
            pairs = []
            for bh in range(BH):
                o = RB[:, :].rearrange("p (t k b o) -> p t b k o", t=BH, k=KY, b=BL)[:, bh, :, KYC * c:KYC * c + KYC]
                i = slot(j)[:, BANK * bh:BANK * (bh + 1)].rearrange("p (b y o) -> p b y o", b=BL, y=KYC)
                pairs.append((o, i))
            return pairs

        def if2_pairs(j):
            g = j - G_IF2
            o = RA[:, :].rearrange("p (t h r k) -> p t k r h", t=BH, h=H, r=2)[:, g // 4, 8 * (g % 4):8 * (g % 4) + 8]
            return [(o, slot(j).rearrange("p (k r h) -> p k r h", k=8, r=2))]

        def t3_pairs(j):
            g = j - G_T3
            return [(RB[:, 1024 * g:1024 * g + 1024], slot(j))]

        def xw_pairs(g, i):
            i = i.rearrange("p (b o i v) -> p i b o v", b=BL, o=4, i=Q)
            return [(XW[:, k, :, 4 * (g % 4):4 * (g % 4) + 4, :].rearrange("p (b t) o v -> p t b o v", t=BH)[:, g // 4],
                     i[:, k]) for k in range(Q)]

        def ln_slot(g):
            return banks(2 * (g % 3), 2)

        def follower_slot(g):
            return ln_slot(g) if g >= 5 else banks(6, 2)

        def lt_pair(l, j):
            g = j - G_LT[l]
            if l == 0:
                return L[0][:, 1024 * g:1024 * g + 1024], slot(j)
            return by_position(L[1])[:, g], slot(j).rearrange("p (j o v) -> p j o v", j=Q, o=HO)

        CW = (E, L2)

        def centred_block(bh, t):
            return blk(RA, (2 * (t // 8) + bh) * 8 + t % 8)

        def row_count(s, t):
            return 127 * (s // 2) + 63 * (s % 2) + t + 1

        def sweep_row(s, q, u):
            if s % 2:
                q, u = HO - 1 - q, Q - 1 - u
            qs = bass.ds(q, 1)
            if s < 2:
                return XW[:, u, :, qs, :].rearrange("p b o v -> p b (o v)")
            return XV[:, u, :, :, qs].rearrange("p b o v -> p b (o v)")

        MOVED = (4, 4, 4, 3, 1)

        def move_rows(eng, n, js):
            o1 = HO - sum(MOVED[:n])
            o0 = o1 - MOVED[n]
            eng.wait_ge(s_arc, 63 + 63 - Q * o0)
            for j in range(Q):
                for i in js:
                    eng.dma_start(XV[C * i:C * i + C, j, :, o0:o1, :],
                                  XW[C * j:C * j + C, i, :, o0:o1, :]).then_inc(s_ph[j], 16)

        def move_out(eng, bls):
            eng.wait_ge(s_arc, 4 * 63)
            for i in range(Q):
                for bl in bls:
                    eng.dma_start(CO[C * bl:C * bl + C, i], XV[C * i:C * i + C, :, BH * bl:BH * bl + BH]
                                  ).then_inc(s_co[i], 16)

        PH = 16 * Q * len(MOVED)

        block = ctx.enter_context(nc.Block())

        @block.sync
        def _(sp):
            for g in range(8):
                sp.dma_start(RA[:, 1024 * g:1024 * g + 1024], x_in[:, 1024 * g:1024 * g + 1024]).then_inc(s_x[g], 16)
            for c in range(2):
                sp.dma_start(RE[:, WCOLS * c:WCOLS * (c + 1)], wspec[c]).then_inc(s_wc[c], 16)
            for o, i in ((conv_sb, conv_w), (convb_sb, conv_b), (gate_sb, gate_w), (gateb_sb, gate_b),
                         (w2_sb, w2), (b2_sb, b2), (own_sb, own)):
                sp.dma_start(o[:], i).then_inc(s_par, 16)
            sp.dma_start(w1_sb[:], w1[0]).then_inc(s_w1[0], 16)
            for c in range(2, NCH):
                if c == 2:
                    sp.wait_ge(s_sum, 8)
                else:
                    sp.wait_ge(s_mix, 4 * (c - 2))
                sp.dma_start(RE[:, WCOLS * (c % 3):WCOLS * (c % 3 + 1)], wspec[c]).then_inc(s_wc[c % 3], 16)
            sp.wait_ge(s_t0, NCH)
            sp.wait_ge(s_t1, NCH)
            sp.dma_start(RC, x_in).then_inc(s_xr, 16)
            sp.wait_ge(s_h, 1)
            sp.dma_start(w1_sb[:], w1[1]).then_inc(s_w1[1], 16)
            for n in range(len(MOVED)):
                move_rows(sp, n, range(0, 2) if n == len(MOVED) - 1 else range(Q))
            move_out(sp, range(0, 2))
            for i in range(Q):
                sp.wait_ge(s_ad, 16 + 4 * (i + 1))
                sp.dma_start(out[:, 2048 * i:2048 * i + 2048], RB[:, 2048 * i:2048 * i + 2048]).then_inc(s_out, 16)
            sp.wait_ge(s_out, 16 * Q)

        @block.gpsimd
        def _(pool):
            pool.memset(RB[:, :], 0.0).then_inc(s_zero, 1)

        @block.tensor
        def _(pe):
            def group(j, ins, rhs):
                for n, lhs in enumerate(ins):
                    if rhs is None:
                        m = pe.transpose(blk(slot(j), n), lhs, ident)
                    else:
                        m = pe.matmul(blk(slot(j), n), lhs, rhs, start=True, stop=True)
                m.then_inc(s_full, 1)

            def norm_tokens(ln, src, follow):
                def follower(g):
                    pe.wait_ge(s_nrm, 8 * ln + g + 1)
                    if 1 <= g < 5:
                        pe.wait_ge(s_fd, 8 * ln + g)
                    follow(g).then_inc(s_ff, 1)

                for g in range(8):
                    if ln == 0:
                        pe.wait_ge(s_x[g], 16)
                    else:
                        pe.wait_ge(s_ad, 16 if g >= 2 else 14 + g)
                    if g >= 3:
                        pe.wait_ge(s_nrm, 8 * ln + g - 2)
                    for n in range(8):
                        m = pe.matmul(blk(ln_slot(g), n), src(g, n), centre, start=True, stop=True)
                    m.then_inc(s_cen, 1)
                    if g >= 3:
                        follower(g - 3)
                for g in range(5, 8):
                    follower(g)

            pe.wait_ge(s_dft, 16)

            def dft_w(g):
                for n in range(8):
                    m = pe.matmul(blk(follower_slot(g), n), blk(RD, 8 * g + n), fwd_w, start=True, stop=True)
                return m

            norm_tokens(0, lambda g, n: blk(RA, 8 * g + n), dft_w)
            for g in range(8):
                if g < 4:
                    pe.wait_ge(s_fd, 8)
                else:
                    wait_one_drained(pe, G_T1 + g - 4)
                group(G_T1 + g, [blk(RC, 8 * g + n) for n in range(8)], None)

            def spectrum(c):
                if c == 0:
                    wait_drained(pe, G_T1 + 7)
                if c >= 2:
                    pe.wait_ge(s_xbd, c - 1)
                    pe.wait_ge(s_xba, c - 1)
                for bh in range(BH):
                    for y in range(KYC):
                        m = pe.matmul(blk(PS[:, 2 * (c % 2) + bh, :], y), blk(RA, bh * KY + c * KYC + y), fwd_h,
                                      start=True, stop=True)
                m.then_inc(s_f2, 1)

            def mix(c):
                pe.wait_ge(s_xbd, c + 1)
                pe.wait_ge(s_xba, c + 1)
                pe.wait_ge(s_wc[c % 3], 16 * (c // 3 + 1))
                for k in range(4):
                    if c >= 1:
                        pe.wait_ge(s_md if k < 2 else s_ma, 2 * (c - 1) + k % 2 + 1)
                    for n in range(8):
                        x, y = divmod(8 * k + n, KYC)
                        for a in range(2):
                            o = PS[64 * a:64 * a + 64, 4 + k, :].rearrange("p (x w y o) -> p x y w o", x=2, w=2, y=KYC)
                            m = pe.matmul(o[:, x % 2, y],
                                          XB[:, c % 2, x, 2 * y + a].rearrange("p r q b -> p (r q b)"),
                                          WR[:, c % 3, a, x, y, :], start=True, stop=True)
                    m.then_inc(s_mix, 1)

            spectrum(0)
            for c in range(NCH):
                if c + 1 < NCH:
                    spectrum(c + 1)
                mix(c)

            for c in range(NCH):
                if c == 0:
                    pe.wait_ge(s_xbd, NCH)
                    pe.wait_ge(s_xba, NCH)
                pe.wait_ge(s_md, 2 * NCH if c else 2)
                pe.wait_ge(s_ma, 2 * NCH if c else 2)
                if c >= 2:
                    pe.wait_ge(s_comb, c - 1)
                    pe.wait_ge(s_tmp, c - 1)
                for w, s in ((0, s_t0), (1, s_t1)):
                    for x in range(X8):
                        m = pe.transpose(blk(banks(4 * (c % 2) + 2 * w, 2), x), Z[:, c, x, w], ident)
                    m.then_inc(s, 1)
            pe.wait_ge(s_comb, NCH)
            pe.wait_ge(s_tmp, NCH)
            for c in range(NCH):
                if c >= 4:
                    wait_one_drained(pe, G_T2 + c - 4)
                group(G_T2 + c, [V_of_b[:, c, :, b] for b in range(B)], None)
            for g in range(8):
                wait_drained(pe, G_T2 + 2 * (g % 4) + 1)
                wait_one_drained(pe, G_IF2 + g - 4)
                group(G_IF2 + g, [blk(RB, 8 * g + n) for n in range(8)], inv_h)
            for g in range(8):
                wait_drained(pe, G_IF2 + (3 if g < 4 else 7))
                wait_one_drained(pe, G_T3 + g - 4)
                group(G_T3 + g, [blk(RA, 8 * g + n) for n in range(8)], None)
            for g in range(8):
                wait_drained(pe, G_T3 + min(g + 4, 7))
                if g >= 4:
                    pe.wait_ge(s_res, g - 3)
                for n in range(8):
                    m = pe.matmul(blk(banks(2 * (g % 4), 2), n), blk(RB, 8 * g + n), inv_w, start=True, stop=True)
                m.then_inc(s_if1, 1)

            pe.wait_ge(s_res, 8)
            pe.wait_ge(s_par, 16 * N_PAR)
            for l in range(2):
                m = pe.matmul(PS[:, l, 0:BL * NE], centre, gate_sb[:, l, :], start=True, stop=True)
            m.then_inc(s_gp, 1)

            def experts(l):
                pe.wait_ge(s_gpc, 3)
                for g in range(8):
                    if l == 1:
                        pe.wait_ge(s_x3, 2 * (g // 2) + 2)
                    if g >= 2:
                        pe.wait_ge(s_sq, EX0[l] + g - 1)
                    for n in range(8):
                        t, bh = 8 * (g // 2) + n, g % 2
                        src = blk(RC, bh * NT + t) if l == 0 else blk(RB, (2 * (t // 2) + bh) * 2 + t % 2)
                        m = pe.matmul(PS[:, 4 * (g % 2) + n // 2, 192 * (n % 2):192 * (n % 2) + 192], src,
                                      proj[:, l, :], start=True, stop=True)
                    m.then_inc(s_pr, 1)
                pe.wait_ge(s_lg, 8 * l + 8)
                for g in range(4):
                    group(G_LT[l] + g, [LT[:, 8 * g + n].rearrange("p h n -> p (h n)") for n in range(8)], None)
                wait_drained(pe, G_LT[l] + 3)
                pe.wait_ge(s_rs, l + 1)
                pe.transpose(PS[0:1, 6, 0:P], rsum[:, :], ident).then_inc(s_rt, 1)

                def pool_tokens(g):
                    pe.wait_ge(s_wtd, 4 * l + g + 1)
                    for t in range(8 * g, 8 * g + 8):
                        for bh in range(BH):
                            m = pe.matmul(PS[:, 4 + bh, 0:P], centred_block(bh, t), WTOK[:, t, :],
                                          start=(t == 0), stop=(t == NT - 1))
                    return m

                for g in range(4):
                    pe.wait_ge(s_ord if l else s_msk, g + 1)
                    if g >= 2:
                        pe.wait_ge(s_wtd, 4 * l + g - 1)
                    for n in range(8):
                        m = pe.transpose(blk(banks(2 * (g % 2), 2), n), blk(CW[l], 8 * g + n), ident)
                    m.then_inc(s_wt, 1)
                    if g == 1:
                        pe.wait_ge(s_rr, l + 1)
                        pe.matmul(PS[0:C, 7, 0:P], ones[:, :], rs_row[:, :], start=True, stop=True).then_inc(s_rb, 1)
                    if g >= 1:
                        pool_tokens(g - 1)
                pool_tokens(3).then_inc(s_pl, 1)
                pe.wait_ge(s_pc, l + 1)
                pe.wait_ge(s_w1[l], 16)
                for e in range(NE):
                    m = pe.matmul(PS[:, 6, B * e:B * e + B], w1_sb[:, e, :], pooled[:, :, e], start=True, stop=True)
                m.then_inc(s_h, 1)
                pe.wait_ge(s_g, l + 1)
                for e in range(NE):
                    m = pe.matmul(PS[0:C, 7, B * e:B * e + B], w2_sb[:, l, e, :], hid[:, e, :], start=True, stop=True)
                m.then_inc(s_o, 1)
                pe.wait_ge(s_ob, l + 1)
                pe.transpose(PS[:, 4, 0:C], eout[:, :, :].rearrange("p b e -> p (b e)"),
                             ident[0:C, 0:C]).then_inc(s_ot, 1)
                pe.wait_ge(s_os, l + 1)
                for k in range(16):
                    if k >= 4:
                        pe.wait_ge(s_ad, 16 * l + k - 3)
                    if l == 0:
                        bh, ch = divmod(k, 8)
                    else:
                        ch, bh = divmod(k, 2)
                    rhs = CW[l][:, ch * BANK:(ch + 1) * BANK]
                    pe.matmul(PS[:, 4 + k % 4, :], espread[:, BL * bh:BL * bh + BL, :].rearrange("p b o -> p (b o)"), rhs,
                              start=True, stop=True).then_inc(s_sc, 1)

            experts(0)

            def turn_rows(g):
                for n in range(8):
                    bl, hb = divmod(n, 2)
                    m = pe.transpose(blk(follower_slot(g), n), blk(RA, 8 * g + BL * hb + bl), ident)
                return m

            norm_tokens(1, lambda g, n: RC[:, 1024 * g + BANK * (n // Q) + n % Q:1024 * g + BANK * (n // Q + 1):Q],
                        turn_rows)

            pe.wait_ge(s_fd, 16)
            for s in range(4):
                def step(q, u):
                    pe.wait_ge(s_st, row_count(s, Q * q + u - 1))
                    for d in range(3):
                        m = pe.matmul(PS[:, u % 2, 0:P].rearrange("p (b v) -> p b v", b=B), conv_sb[:, s, d, :],
                                      state[:, (u + 1 + s) % 2, :, d:d + HO], start=(d == 0), stop=(d == 2))
                    m.then_inc(s_cv, 1)
                    for _ in range(4):
                        pe.matmul(PS[:, 2, 0:P], warm[:, :], warm[:, :], start=True, stop=True)

                for u in range(1, Q):
                    step(0, u)
                with pe.Fori(1, HO) as q:
                    for u in range(Q):
                        step(q, u)

            experts(1)

        @block.scalar
        def _(act):
            act.dma_start(dft_sb[:], dft).then_inc(s_dft, 16)

            def root(n, first, width, eps):
                act.wait_ge(s_sum, n + 1)
                act.activation(std[:, first:first + width], sums[:, first:first + width], ACT.Sqrt, bias=eps,
                               scale=1.0 / C).then_inc(s_std, 1)

            def norm_tokens(ln, pairs):
                def drain_follower(g):
                    act.wait_ge(s_ff, 8 * ln + g + 1)
                    for o, i in pairs(g, follower_slot(g)):
                        m = act.copy(o, i)
                    m.then_inc(s_fd, 1)

                for g in range(8):
                    act.wait_ge(s_cen, 8 * ln + g + 1)
                    if LN0[ln] + g >= 2:
                        act.wait_ge(s_sum, LN0[ln] + g - 1)
                    act.activation(square[:, g % 2, 0:1024], ln_slot(g), ACT.Square).then_inc(s_sq, 1)
                    if g >= 1:
                        root(LN0[ln] + g - 1, 32 * (g - 1), 32, eps_sb[:, 0:1])
                    if g >= 4:
                        drain_follower(g - 4)
                root(LN0[ln] + 7, 224, 32, eps_sb[:, 0:1])
                for g in range(4, 8):
                    drain_follower(g)

            def drain(j, pairs):
                act.wait_ge(s_full, j + 1)
                for o, i in pairs(j):
                    m = act.copy(o, i)
                m.then_inc(s_da, 1)

            act.wait_ge(s_set, N_SET)
            norm_tokens(0, f1_pairs)
            for j in range(G_T1, G_T1 + 8, 2):
                drain(j, t1_pairs)

            def spread(c):
                act.wait_ge(s_f2, c + 1)
                if c == 0:
                    act.wait_ge(s_zero, 1)
                if c >= 2:
                    act.wait_ge(s_mix, 4 * (c - 1))
                for o, i in xb_pairs(c, 1):
                    m = act.copy(o, i)
                m.then_inc(s_xba, 1)

            spread(0)
            for c in range(NCH):
                if c + 1 < NCH:
                    spread(c + 1)
                for k in (2, 3):
                    act.wait_ge(s_mix, 4 * c + k + 1)
                    act.copy(z_bank(c, k), PS[:, 4 + k, :]).then_inc(s_ma, 1)
            for c in range(NCH):
                act.wait_ge(s_t1, c + 1)
                if c >= 2:
                    act.wait_ge(s_comb, c - 1)
                act.copy(imtmp[:, c % 2, :], banks(4 * (c % 2) + 2, 2)).then_inc(s_tmp, 1)
            for j in range(G_T2, G_T2 + 8, 2):
                drain(j, t2_pairs)
            for j in range(G_IF2, G_IF2 + 8, 2):
                drain(j, if2_pairs)
            for j in range(G_T3, G_T3 + 8, 2):
                drain(j, t3_pairs)

            def experts(l):
                for g in range(8):
                    act.wait_ge(s_pr, 8 * l + g + 1)
                    xc = PS[:, 4 * (g % 2):4 * (g % 2) + 4, 0:384].rearrange("p k (j n) -> p k j n", j=2)[:, :, :, 0:P]
                    t0, bh = 8 * (g // 2), g % 2
                    raw = PS[:, 4 * (g % 2):4 * (g % 2) + 4, 0:384].rearrange("p k (j n) -> p k j n", j=2)[:, :, :, P:]
                    act.copy(LT[:, t0:t0 + 8, bh, :].rearrange("p (k j) n -> p k j n", j=2), raw)
                    act.copy(RA[:, 1024 * g:1024 * g + 1024].rearrange("p (k j n) -> p k j n", k=4, j=2), xc)
                    act.wait_ge(s_sum, EX0[l] + g - 1)
                    act.activation(square[:, g % 2, 0:1024].rearrange("p (k j n) -> p k j n", k=4, j=2), xc,
                                   ACT.Square).then_inc(s_sq, 1)
                    if g >= 1:
                        root(EX0[l] + g - 1, 32 * (g - 1), 32, eps_sb[:, 1:2])
                root(EX0[l] + 7, 224, 32, eps_sb[:, 1:2])
                for j in (G_LT[l], G_LT[l] + 2):
                    act.wait_ge(s_full, j + 1)
                    o, i = lt_pair(l, j)
                    act.activation(o, i, ACT.Identity, bias=gateb_sb[:, l:l + 1]).then_inc(s_da, 1)
                act.wait_ge(s_nm, l + 1)
                act.activation(E, L[l], ACT.Exp, bias=negmax[:, :], accum_out=expsum[:, :]).then_inc(s_exp, 1)
                if l == 1:
                    for i in range(Q):
                        act.wait_ge(s_msk, 8)
                        act.copy(CW[1][:, 1024 * i:1024 * i + 1024].rearrange("p (j o v) -> p j o v", j=Q, o=HO),
                                 by_position(E)[:, i]).then_inc(s_ord, 1)
                act.wait_ge(s_rt, l + 1)
                act.copy(rs_row[:, :], PS[0:1, 6, 0:P]).then_inc(s_rr, 1)
                act.wait_ge(s_rb, l + 1)
                act.copy(rs_rep[:, :], PS[0:C, 7, 0:P]).then_inc(s_rp, 1)
                act.wait_ge(s_h, l + 1)
                act.activation(hid[:, :, :].rearrange("p e b -> p (e b)"), PS[:, 6, 0:P], ACT.Gelu).then_inc(s_g, 1)

            act.wait_ge(s_par, 16 * N_PAR)
            experts(0)

            norm_tokens(1, xw_pairs)

            for s in range(4):
                def fetch(s, q, u):
                    act.activation(rowb[:, u], sweep_row(s, q, u), ACT.Identity,
                                   bias=convb_sb[:, s:s + 1]).then_inc(s_row, 1)

                def archive(q, u):
                    act.copy(sweep_row(s, q, u), state[:, (u + s) % 2, :, 1:1 + HO]).then_inc(s_arc, 1)

                def step(q, u):
                    act.wait_ge(s_st, row_count(s, Q * q + u))
                    fetch(s, q + (u + 1) // Q, (u + 1) % Q)
                    archive(q, u)

                if s == 0:
                    act.wait_ge(s_fd, 16)
                    fetch(s, 0, 1)
                elif s == 2:
                    move_rows(act, len(MOVED) - 1, range(2, Q))
                    act.wait_ge(s_ph[1], PH)
                    fetch(s, 0, 1)
                for u in range(1, Q):
                    if s == 2 and u < Q - 1:
                        act.wait_ge(s_ph[u + 1], PH)
                    step(0, u)
                with act.Fori(1, HO - 1) as q:
                    for u in range(Q):
                        step(q, u)
                for u in range(Q - 1):
                    step(HO - 1, u)
                act.wait_ge(s_st, row_count(s, H - 1))
                if s % 2 == 0:
                    act.wait_ge(s_arc, 63 * s + 62)
                    fetch(s + 1, 0, 1)
                archive(HO - 1, Q - 1)
            move_out(act, range(2, BL))

            experts(1)

        @block.vector
        def _(dve):
            dve.memset(eps_sb[:, 0:1], LN_C_EPS[0]).then_inc(s_set, 1)
            dve.memset(eps_sb[:, 1:2], LN_T_EPS).then_inc(s_set, 1)
            dve.memset(state[:, :, :, :], 0.0).then_inc(s_set, 1)
            dve.memset(ones[:, :], 1.0).then_inc(s_set, 1)
            dve.memset(pooled[C:C + 1, :, :], 1.0).then_inc(s_set, 1)
            dve.memset(warm[:, :], 0.0).then_inc(s_set, 1)

            def norm_tokens(ln):
                def total(g):
                    dve.wait_ge(s_sq, LN0[ln] + g + 1)
                    dve.tensor_reduce(sums[:, 32 * g:32 * g + 32],
                                      square[:, g % 2, 0:1024].rearrange("p (a c) -> p a c", c=C), AX_X,
                                      ALU.add).then_inc(s_sum, 1)

                total(0)
                for g in range(8):
                    if g < 7:
                        total(g + 1)
                    r = rstd[:, 32 * g:32 * g + 32]
                    dve.wait_ge(s_std, LN0[ln] + g + 1)
                    dve.reciprocal(r, std[:, 32 * g:32 * g + 32]).then_inc(s_rec, 1)
                    dve.wait_ge(s_rec, LN0[ln] + g + 1)
                    if ln == 0:
                        m = dve.tensor_tensor(RD[:, 1024 * g:1024 * g + 1024].rearrange("p (a c) -> p a c", c=C),
                                              ln_slot(g).rearrange("p (a c) -> p a c", c=C),
                                              r.unsqueeze(2).to_broadcast([P, 32, C]), ALU.mult)
                    else:
                        for hb in range(2):
                            k = slice(BANK * hb, BANK * (hb + 1))
                            m = dve.tensor_tensor(
                                RA[:, 1024 * g:1024 * g + 1024][:, k].rearrange("p (b j c) -> p j b c", b=BL, j=Q),
                                ln_slot(g)[:, k].rearrange("p (j b c) -> p j b c", b=BL, j=Q),
                                r[:, 16 * hb:16 * hb + 16].rearrange("p (j b) -> p j b", b=BL).unsqueeze(3)
                                .to_broadcast([P, Q, BL, C]), ALU.mult)
                    m.then_inc(s_nrm, 1)

            def drain(j, pairs):
                dve.wait_ge(s_full, j + 1)
                for o, i in pairs(j):
                    m = dve.tensor_copy(o, i)
                m.then_inc(s_dd, 1)

            norm_tokens(0)
            for j in range(G_T1 + 1, G_T1 + 8, 2):
                drain(j, t1_pairs)

            def spread(c):
                dve.wait_ge(s_f2, c + 1)
                if c == 0:
                    dve.wait_ge(s_zero, 1)
                if c >= 2:
                    dve.wait_ge(s_mix, 4 * (c - 1))
                for o, i in xb_pairs(c, 0):
                    m = dve.tensor_copy(o, i)
                m.then_inc(s_xbd, 1)

            spread(0)
            for c in range(NCH):
                if c + 1 < NCH:
                    spread(c + 1)
                for k in (0, 1):
                    dve.wait_ge(s_mix, 4 * c + k + 1)
                    dve.tensor_copy(z_bank(c, k), PS[:, 4 + k, :]).then_inc(s_md, 1)
            for c in range(NCH):
                dve.wait_ge(s_t0, c + 1)
                dve.wait_ge(s_tmp, c + 1)
                by_re = banks(4 * (c % 2), 2).rearrange("p (x a r n) -> p x a r n", x=X8, a=2, r=2)
                by_im = imtmp[:, c % 2, :].rearrange("p (x a r n) -> p x a r n", x=X8, a=2, r=2)
                dve.tensor_tensor(V[:, c, :, :, 0, :], by_re[:, :, :, 0, :], by_im[:, :, :, 1, :], ALU.subtract)
                dve.tensor_tensor(V[:, c, :, :, 1, :], by_re[:, :, :, 1, :], by_im[:, :, :, 0, :],
                                  ALU.add).then_inc(s_comb, 1)
            for j in range(G_T2 + 1, G_T2 + 8, 2):
                drain(j, t2_pairs)
            for j in range(G_IF2 + 1, G_IF2 + 8, 2):
                drain(j, if2_pairs)
            for j in range(G_T3 + 1, G_T3 + 8, 2):
                drain(j, t3_pairs)
            dve.wait_ge(s_xr, 16)
            for g in range(8):
                dve.wait_ge(s_if1, g + 1)
                x1 = RC[:, 1024 * g:1024 * g + 1024]
                dve.tensor_tensor(x1, banks(2 * (g % 4), 2), x1, ALU.add).then_inc(s_res, 1)

            dve.wait_ge(s_par, 16 * N_PAR)
            dve.tensor_scalar(negb_sb[:, :], convb_sb[:, :], -1.0, None, ALU.mult).then_inc(s_gpc, 1)
            dve.tensor_copy(proj[:, :, 0:P], centre.unsqueeze(1).to_broadcast([P, 2, P])).then_inc(s_gpc, 1)
            dve.wait_ge(s_gp, 1)
            dve.tensor_copy(proj[:, :, P:], PS[:, 0:2, 0:BL * NE]).then_inc(s_gpc, 1)

            def experts(l):
                def total(g):
                    dve.wait_ge(s_sq, EX0[l] + g + 1)
                    dve.tensor_reduce(sums[:, 32 * g:32 * g + 32],
                                      square[:, g % 2, 0:1024].rearrange("p (a c) -> p a c", c=C), AX_X,
                                      ALU.add).then_inc(s_sum, 1)

                def scale(g):
                    t0, bh = 8 * (g // 2), g % 2
                    r = rstd[:, :].rearrange("p (t h b) -> p h t b", h=BH, b=BL)[:, bh, t0:t0 + 8, :]
                    dve.wait_ge(s_std, EX0[l] + g + 1)
                    dve.reciprocal(r, std[:, 32 * g:32 * g + 32].rearrange("p (t b) -> p t b", b=BL)
                                   ).then_inc(s_rec, 1)
                    dve.wait_ge(s_rec, EX0[l] + g + 1)
                    lt = LT[:, t0:t0 + 8, bh, :].rearrange("p t (b e) -> p t b e", e=NE)
                    dve.tensor_tensor(lt, lt, r.unsqueeze(3).to_broadcast([P, 8, BL, NE]), ALU.mult).then_inc(s_lg, 1)

                total(0)
                for g in range(8):
                    if g < 7:
                        total(g + 1)
                    scale(g)
                for j in (G_LT[l] + 1, G_LT[l] + 3):
                    dve.wait_ge(s_full, j + 1)
                    o, i = lt_pair(l, j)
                    dve.tensor_scalar(o, i, gateb_sb[:, l:l + 1], None, ALU.add).then_inc(s_dd, 1)
                wait_drained(dve, G_LT[l] + 3)
                dve.max(top8[:, :], L[l]).then_inc(s_mx, 1)
                dve.wait_ge(s_mx, l + 1)
                dve.tensor_scalar(negmax[:, :], top8[:, 0:1], -1.0, None, ALU.mult).then_inc(s_nm, 1)
                dve.match_replace(L2, top8[:, :], L[l], MASKED).then_inc(s_rep, 1)
                dve.wait_ge(s_exp, l + 1)
                dve.reciprocal(rsum[:, :], expsum[:, :]).then_inc(s_rs, 1)
                dve.wait_ge(s_rep, l + 1)
                for g in range(4):
                    c = slice(1024 * g, 1024 * g + 1024)
                    dve.scalar_tensor_tensor(out=E[:, c], in0=L2[:, c], scalar=MASKED / 2, in1=E[:, c],
                                             op0=ALU.is_le, op1=ALU.mult).then_inc(s_msk, 1)
                for g in range(4):
                    dve.wait_ge(s_wt, 4 * l + g + 1)
                    dve.tensor_tensor(WTOK[:, 8 * g:8 * g + 8, :].rearrange("p t (b e) -> p (t b) e", e=NE),
                                      banks(2 * (g % 2), 2).rearrange("p (a e) -> p a e", e=NE),
                                      rstd[:, 64 * g:64 * g + 64].unsqueeze(2).to_broadcast([P, 64, NE]),
                                      ALU.mult).then_inc(s_wtd, 1)
                dve.wait_ge(s_pl, l + 1)
                dve.wait_ge(s_rp, l + 1)
                for b in range(B):
                    bh, bl = divmod(b, BL)
                    m = dve.tensor_tensor(pooled[0:C, b, :], PS[C * bl:C * bl + C, 4 + bh, NE * b:NE * b + NE],
                                          rs_rep[:, NE * b:NE * b + NE], ALU.mult)
                m.then_inc(s_pc, 1)
                dve.wait_ge(s_o, l + 1)
                dve.tensor_tensor(eout[:, :, :].rearrange("p b e -> p e b"),
                                  PS[0:C, 7, 0:P].rearrange("p (e b) -> p e b", b=B),
                                  b2_sb[:, l, :].unsqueeze(2).to_broadcast([C, NE, B]), ALU.add).then_inc(s_ob, 1)
                dve.wait_ge(s_ot, l + 1)
                dve.scalar_tensor_tensor(out=espread[:, :, :],
                                         in0=PS[:, 4, 0:C].unsqueeze(1).to_broadcast([P, B, C]),
                                         scalar=rsum[:, :], in1=own_sb[:, :].unsqueeze(2).to_broadcast([P, B, C]),
                                         op0=ALU.mult, op1=ALU.mult).then_inc(s_os, 1)
                for k in range(16):
                    dve.wait_ge(s_sc, 16 * l + k + 1)
                    if l == 0:
                        x2 = RC[:, BANK * k:BANK * (k + 1)]
                        dve.tensor_tensor(x2, PS[:, 4 + k % 4, :], x2, ALU.add).then_inc(s_ad, 1)
                    else:
                        i, j, bh = k // 4, k // 2 % 2 * 2, k % 2
                        x4 = X3[:, i, j:j + 2, bh].rearrange("p j o v -> p j (o v)")
                        dve.tensor_tensor(x4, PS[:, 4 + k % 4, :].rearrange("p (j n) -> p j n", j=2), x4,
                                          ALU.add).then_inc(s_ad, 1)

            experts(0)

            norm_tokens(1)

            for s in range(4):
                if s % 2 == 0:
                    if s == 0:
                        dve.wait_ge(s_fd, 16)
                    else:
                        dve.wait_ge(s_ph[0], PH)
                    dve.tensor_copy(state[:, 0, :, 1:1 + HO], sweep_row(s, 0, 0)).then_inc(s_st, 1)

                def step(q, u):
                    dve.wait_ge(s_cv, 63 * s + Q * q + u)
                    dve.wait_ge(s_row, 63 * s + Q * q + u)
                    dve.scalar_tensor_tensor(out=state[:, (u + s) % 2, :, 1:1 + HO],
                                             in0=PS[:, u % 2, 0:P].rearrange("p (b v) -> p b v", b=B),
                                             scalar=negb_sb[:, s:s + 1], in1=rowb[:, u],
                                             op0=ALU.max, op1=ALU.add).then_inc(s_st, 1)

                for u in range(1, Q):
                    step(0, u)
                with dve.Fori(1, HO) as q:
                    for u in range(Q):
                        step(q, u)

            for k in range(8):
                i, bh = divmod(k, 2)
                dve.wait_ge(s_co[i], 16 * BL)
                dve.tensor_tensor(X3[:, i, :, bh], CO[:, i, :, bh],
                                  by_position(RC[:, TOK * bh:TOK * (bh + 1)])[:, i], ALU.add).then_inc(s_x3, 1)

            experts(1)


def dft_tables():
    f = np.float64
    centre = np.eye(P, dtype=f) - np.kron(np.eye(BL), np.full((C, C), 1.0 / C))
    w, ky = np.arange(W), np.arange(KY)
    a = 2 * np.pi * np.outer(w, ky) / W
    fwd_w = np.kron(np.eye(2), np.concatenate([np.cos(a), -np.sin(a)], 1) / W)
    h, kx = np.arange(H), np.arange(H)
    a = 2 * np.pi * np.outer(h, kx) / H
    c, s = np.cos(a), np.sin(a)
    full = np.array([[c, -s], [s, c]]) / H
    fwd_h = full.transpose(0, 2, 3, 1).reshape(2, H, 2, Q, X8, 2)
    fwd_h = fwd_h.transpose(0, 1, 2, 3, 5, 4).reshape(P, P)
    inv = np.array([[c, s], [-s, c]])
    inv_h = inv.transpose(3, 0, 1, 2).reshape(2, Q, X8, 2, 2, H)
    inv_h = inv_h.transpose(2, 0, 3, 1, 4, 5).reshape(P, P)
    a = 2 * np.pi * np.outer(ky, w) / W
    twice = np.where(ky == 0, 1.0, 2.0)[:, None]
    inv_w = np.kron(np.eye(2), np.concatenate([twice * np.cos(a), -twice * np.sin(a)], 0))
    return np.ascontiguousarray(np.stack([centre, np.eye(P), fwd_w, fwd_h, inv_h, inv_w], 1).astype(np.float32))


def banded(w):
    m = np.zeros((Q, C, 3, Q, C), w.dtype)
    for d in range(3):
        for i in range(Q):
            for j in range(Q):
                k = Q * (d - 1) + i - j + TAPS // 2
                if 0 <= k < TAPS:
                    m[i, :, d, j, :] = w[:, :, k].T
    return m.reshape(P, 3, P)


def kernel(**inputs):
    import concourse.bacc as bacc
    from concourse.bass_utils import run_bass_kernel_spmd

    a = {k: np.asarray(v) for k, v in inputs.items()}
    x = a["x"].reshape(BH, BL, C, TOK).transpose(1, 2, 0, 3).reshape(P, NF)
    ws = np.stack([np.stack([a[f"L0_conv_w{n}_{p}"] for p in ("real", "imag")]) for n in (1, 2)])
    ws = ws.reshape(2, 2, C, C, Q, X8, NCH, KYC).transpose(6, 4, 2, 0, 5, 7, 1, 3).reshape(NCH, P, WCOLS)
    conv_w = np.stack([banded(a[f"L1_conv_w_{s}"]) for s in "durl"], 1)
    conv_b = np.stack([np.tile(a[f"L1_conv_b_{s}"], Q) for s in "durl"], 1)
    gate = np.zeros((BL, C, 2, BL, NE), np.float32)
    for l in range(2):
        for b in range(BL):
            gate[b, :, l, b, :] = a[f"L{l}_ffn_gate_w"].T
    gate_b = np.stack([np.tile(a[f"L{l}_ffn_gate_b"], B) for l in range(2)], 1)
    w1 = np.stack([a[f"L{l}_ffn_weight1"].transpose(1, 0, 2) for l in range(2)])
    w2 = np.stack([a[f"L{l}_ffn_weight2"][:, :NHID].transpose(1, 0, 2) for l in range(2)], 1)
    b2 = np.stack([a[f"L{l}_ffn_weight2"][:, NHID].T for l in range(2)], 1)
    own = np.repeat(np.eye(B, dtype=np.float32), NE, 0)
    arrays = {"x_in": x, "dft": dft_tables(), "wspec": ws, "conv_w": conv_w, "conv_b": conv_b,
              "gate_w": gate.reshape(P, 2, BL * NE), "gate_b": gate_b, "w1": w1, "w2": w2, "b2": b2, "own": own}
    arrays = {k: np.ascontiguousarray(v) for k, v in arrays.items()}

    nc = bacc.Bacc("TRN2", target_bir_lowering=False, num_devices=1)
    args = [nc.dram_tensor(k, v.shape, F32, kind="ExternalInput").ap() for k, v in arrays.items()]
    args.append(nc.dram_tensor("out", (P, NF), F32, kind="ExternalOutput").ap())
    build_kernel(nc, *args)
    r = run_bass_kernel_spmd(nc, [arrays], core_ids=[0])
    y = np.asarray(r.results[0]["out"])
    y = y.reshape(BL, C, Q, Q, BH, HO, HO).transpose(4, 0, 1, 5, 2, 6, 3)
    return np.ascontiguousarray(y.reshape(B, C, H, W))
```

```python
from contextlib import ExitStack

import numpy as np

import concourse.bass as bass
from concourse import mybir

B, C, H, W = 8, 32, 64, 64
P = 128
BL, BH = P // C, B * C // P
TOK = H * W
KY = W // 2
NE, NHID = 16, 128
Q = 4
HO = H // Q
TAPS = 9
NT = TOK // P
BANK = 512
NW = 4
WRUN = W // NW
KYC = 4
NCH = KY // KYC
X8 = H // 2 // Q
WCOLS = 2 * X8 * KYC * 2 * C
NF = BH * TOK
LN_C_EPS, LN_T_EPS = (1e-6, 1e-6), 1e-5
MASKED = -3.0e38

F32 = mybir.dt.float32
BF16 = mybir.dt.bfloat16
ALU = mybir.AluOpType
ACT = mybir.ActivationFunctionType
AX_X = mybir.AxisListType.X


def build_kernel(nc, x_in, dft, wspec, conv_w, conv_b, gate_w, gate_b, w1, w2, b2, own, out):
    with ExitStack() as ctx:
        def sb(name, shape, dt=F32):
            return ctx.enter_context(nc.sbuf_tensor(name, shape, dt))

        def sem(name):
            return ctx.enter_context(nc.semaphore(name))

        RA, RB, RCD = sb("RA", [P, NF]), sb("RB", [P, NF]), sb("RCD", [P, 2 * NF])
        RC, RD = RCD[:, 0:NF], RCD[:, NF:2 * NF]
        RE = sb("RE", [P, 3 * WCOLS])
        PS = ctx.enter_context(nc.psum_tensor("PS", [P, 8, BANK], F32))

        dft_sb = sb("dft_sb", [P, 6, P])
        centre, ident, fwd_w, fwd_h, inv_h, inv_w = (dft_sb[:, i, :] for i in range(6))
        own_sb = sb("own_sb", [P, B])
        conv_sb = sb("conv_sb", [P, 4, 3, P])
        convb_sb, negb_sb = sb("convb_sb", [P, 4]), sb("negb_sb", [P, 4])
        gate_sb = sb("gate_sb", [P, 2, BL * NE])
        proj = sb("proj", [P, 2, P + BL * NE])
        gateb_sb = sb("gateb_sb", [P, 2])
        w1_sb = sb("w1_sb", [C + 1, NE, NHID])
        w2_sb, b2_sb = sb("w2_sb", [P, 2, NE, C]), sb("b2_sb", [C, 2, NE])
        eps_sb = sb("eps_sb", [P, 2])
        sums, std, rstd = sb("sums", [P, 256]), sb("std", [P, 256]), sb("rstd", [P, 256])
        cand, top8 = sb("cand", [P, 4 * 8]), sb("top8", [P, 8])
        negmax, expsum, rsum = sb("negmax", [P, 1]), sb("expsum", [P, 1]), sb("rsum", [P, 1])
        ones = sb("ones", [1, C])
        rs_row, rs_rep = sb("rs_row", [1, P]), sb("rs_rep", [C, P])
        pooled = sb("pooled", [C + 1, B, NE])
        hid = sb("hid", [P, NE, B])
        eout = sb("eout", [C, B, NE])
        espread = sb("espread", [P, B, C])
        state = sb("state", [P, 2, B, HO + 2])
        warm = sb("warm", [P, P], BF16)

        s_x = [sem(f"x_loaded{i}") for i in range(8)]
        s_dft, s_par = sem("dft_loaded"), sem("params_loaded")
        s_w1 = [sem(f"w1_loaded{i}") for i in range(2)]
        s_wc = [sem(f"wspec_loaded{i}") for i in range(3)]
        s_xr = sem("x_reloaded")
        s_set, s_zero = sem("memsets_done"), sem("xb_zeroed")
        s_gp, s_gpc = sem("gate_projected"), sem("gate_copied")
        s_cen, s_sq, s_sum = sem("ln_centred"), sem("squared"), sem("summed")
        s_xc, s_sqp = sem("centred_copied"), sem("squared_pool")
        s_std, s_rec, s_nrm = sem("std_ready"), sem("rstd_ready"), sem("ln_normed")
        s_full, s_da, s_dd = sem("group_full"), sem("group_drained_act"), sem("group_drained_dve")
        s_f2, s_xba, s_xbd = sem("spectrum_full"), sem("xb_written_act"), sem("xb_written_dve")
        s_mix, s_ma, s_md = sem("mixed"), sem("mix_drained_act"), sem("mix_drained_dve")
        s_t0, s_t1 = sem("products_re_turned"), sem("products_im_turned")
        s_tmp, s_comb = sem("products_im_copied"), sem("products_combined")
        s_tf, s_td = sem("turned_full"), sem("turned_drained")
        s_df, s_dr = sem("dft_h_full"), sem("dft_h_drained")
        s_if1, s_res = sem("image_full"), sem("residual_added")
        s_pr, s_lg = sem("projected"), sem("logits_scaled")
        s_ld, s_pm = sem("logits_drained"), sem("top8_of_quarter")
        s_mx, s_nm, s_rep = sem("top8_found"), sem("negmax_ready"), sem("top8_replaced")
        s_exp, s_rs, s_msk = sem("exps_ready"), sem("rsum_ready"), sem("weights_masked")
        s_ord = sem("weights_ordered")
        s_wt, s_wtd = sem("weights_turned"), sem("weights_scaled")
        s_rt, s_rr = sem("rsum_turned"), sem("rsum_row_copied")
        s_rb, s_rp = sem("rsum_spread"), sem("rsum_rep_copied")
        s_pl, s_pc = sem("pooled_full"), sem("pooled_copied")
        s_h, s_g = sem("hidden_full"), sem("gelu_done")
        s_o, s_ob = sem("experts_full"), sem("experts_biased")
        s_ot, s_os = sem("experts_turned"), sem("experts_spread")
        s_sc, s_ad = sem("scatter_full"), sem("scatter_added")
        s_ff, s_fd = sem("follower_full"), sem("follower_drained")
        s_st, s_cv = sem("state_ready"), sem("conv_ready")
        s_row, s_arc = sem("row_fetched"), sem("row_archived")
        s_ph = [sem(f"columns_in{j}") for j in range(Q)]
        s_php = [sem(f"columns_in_pool{j}") for j in range(Q)]
        s_co = [sem(f"conv_out{i}") for i in range(NW)]
        s_cop = sem("conv_out_pool")
        s_x3, s_x3d, s_out = sem("conv_added_pool"), sem("conv_added_dve"), sem("stored")
        N_SET, N_PAR = 6, 7

        def blk(region, n):
            return region[:, n * P:(n + 1) * P]

        def banks(b0, nb):
            return PS[:, b0:b0 + nb, :].rearrange("p k c -> p (k c)")

        XB = RB[:, :].rearrange("p (s x z r q b) -> p s x z r q b", s=2, x=X8, z=2 * KYC, r=2, q=Q)
        Z = RCD[:, :].rearrange("p (c x w n) -> p c x w n", c=NCH, x=X8, w=2)
        V = RA[:, :].rearrange("p (c x a r n) -> p c x a r n", c=NCH, x=X8, a=2, r=2)
        V_of_b = RA[:, :].rearrange("p (c m b) -> p c m b", c=NCH, b=B)
        WR = RE[:, :].rearrange("p (s a x y n) -> p s a x y n", s=3, a=2, x=X8, y=KYC)
        imtmp = RE[:, 0:2 * 1024].rearrange("p (s n) -> p s n", s=2)
        square = RE[:, 2 * WCOLS:3 * WCOLS].rearrange("p (s n) -> p s n", s=2)
        LT = RD[:, 0:TOK].rearrange("p (t h n) -> p t h n", h=BH, t=NT)
        L = (RB[:, 0:TOK], RC[:, 0:TOK])
        L2, E = RD[:, 0:TOK], RD[:, TOK:2 * TOK]
        WTOK = RE[:, 0:WCOLS].rearrange("p (t n) -> p t n", t=NT)
        XW = RD.rearrange("p (i b o v) -> p i b o v", i=Q, b=B, o=HO)
        XV = RE[:, 0:NF].rearrange("p (j b o v) -> p j b o v", j=Q, b=B, o=HO)
        XF = RB[:, :].rearrange("p (v j b o) -> p (v j) b o", v=HO, j=Q, b=B)
        CO = RD.rearrange("p (k i w t o) -> p k i w t o", k=NW, i=Q, w=WRUN, t=BH)
        X3 = RA[:, :].rearrange("p (k t i w o) -> p k t i w o", k=NW, t=BH, i=Q, w=WRUN)

        rowb = RE[:, NF:NF + 4 * P].rearrange("p (s b v) -> p s b v", s=4, b=B)

        def by_run(ap, k):
            return ap.rearrange("p (o i w) -> p i w o", o=HO, i=Q)[:, :, W - WRUN * (k + 1):W - WRUN * k, :]

        G_T1 = 0
        G_LT = (8, 12)
        LN0, EX0 = (0, 16), (8, 24)
        POOL_GROUPS = (1, 3, 5)
        LNS, EXS = (0, 13), (8, 21)

        def slot(j):
            return banks(2 * (j % 4), 2)

        def wait_drained(eng, j):
            eng.wait_ge(s_da, j // 2 + 1)
            if j >= 1:
                eng.wait_ge(s_dd, (j + 1) // 2)

        def wait_one_drained(eng, j):
            eng.wait_ge(s_dd if j % 2 else s_da, j // 2 + 1)

        def turn_slot(g):
            return banks(2 * (g % 2), 2)

        def dft_slot(g):
            return banks(4 + 2 * (g % 2), 2)

        def f1_pairs(g, i):
            o = RC.rearrange("p (t k r h) -> p t h r k", t=BH, k=KY, r=2)[:, g // 4, 16 * (g % 4):16 * (g % 4) + 16]
            return [(o, i.rearrange("p (h r k) -> p h r k", r=2, k=KY))]

        def t1_pairs(j):
            g = j - G_T1
            return [(RA[:, 1024 * g:1024 * g + 1024], slot(j))]

        def xb_pairs(c, bh):
            pairs = []
            for bl in range(BL):
                for q in range(Q):
                    i = PS[C * bl:C * bl + C, 2 * (c % 2) + bh, :].rearrange("p (z q r x) -> p q z r x", q=Q, r=2, x=X8)
                    o = XB[C * q:C * q + C, c % 2, :, :, :, q, bh * BL + bl].rearrange("p x z r -> p z r x")
                    pairs.append((o, i[:, q]))
            return pairs

        def z_bank(c, k):
            return RCD[:, 2048 * c + BANK * k:2048 * c + BANK * (k + 1)]

        def t2_pairs(c):
            pairs = []
            for bh in range(BH):
                o = RB[:, :].rearrange("p (t k b o) -> p t b k o", t=BH, k=KY, b=BL)[:, bh, :, KYC * c:KYC * c + KYC]
                i = turn_slot(c)[:, BANK * bh:BANK * (bh + 1)].rearrange("p (b y o) -> p b y o", b=BL, y=KYC)
                pairs.append((o, i))
            return pairs

        def if2_pairs(g):
            o = RD.rearrange("p (t h r k) -> p t k r h", t=BH, h=H, r=2)[:, g % 2, 8 * (g // 2):8 * (g // 2) + 8]
            return [(o, dft_slot(g).rearrange("p (k r h) -> p k r h", k=8, r=2))]

        def t3_pairs(g):
            return [(RB[:, 1024 * g:1024 * g + 1024], turn_slot(g))]

        def xw_pairs(g, i):
            i = i.rearrange("p (b o i v) -> p i b o v", b=BL, o=4, i=Q)
            return [(XW[:, k, :, 4 * (g % 4):4 * (g % 4) + 4, :].rearrange("p (b t) o v -> p t b o v", t=BH)[:, g // 4],
                     i[:, k]) for k in range(Q)]

        FED = (5, 9)

        def ln_slot(g):
            return banks(2 * (g % 4), 2)

        def lt_pair(l, j):
            g = j - G_LT[l]
            if l == 0:
                return L[0][:, 1024 * g:1024 * g + 1024], slot(j)
            return by_run(L[1], g), slot(j).rearrange("p (i w o) -> p i w o", i=Q, w=WRUN)

        def part(x, l, g):
            if l == 0:
                return x[:, 1024 * g:1024 * g + 1024]
            return x.rearrange("p (h w) -> p h w", w=W)[:, :, W - WRUN * (g + 1):W - WRUN * g]

        CW = (E, RC[:, TOK:2 * TOK])

        def centred(l, g):
            return RB[:, 1024 * (7 - g):1024 * (8 - g)] if l else RA[:, 1024 * g:1024 * g + 1024]

        def row_count(s, t):
            return 127 * (s // 2) + 63 * (s % 2) + t + 1

        def row_at(image, s, q, u):
            if s % 2:
                q, u = HO - 1 - q, Q - 1 - u
            if image is XF:
                return XF[:, bass.ds(Q * q + u, 1)].rearrange("p a b o -> p (a b) o")
            qs = bass.ds(q, 1)
            if image is XW:
                return XW[:, u, :, qs, :].rearrange("p b o v -> p b (o v)")
            return XV[:, u, :, :, qs].rearrange("p b o v -> p b (o v)")

        SRC, DST = (XW, XW, XV, XF), (XW, XW, XF, XF)

        MOVED = (5, 5, 4, 2)
        def on_pool(n, m):
            return m == 3 or (m == 2 and n % 2 == 0)

        def wait_columns(eng, j):
            share = sum(on_pool(j, i) for i in range(Q))
            eng.wait_ge(s_ph[j], 16 * (Q * len(MOVED) - share))
            eng.wait_ge(s_php[j], 16 * share)

        def move_rows(eng, n, mine, sems):
            o1 = HO - sum(MOVED[:n])
            o0 = o1 - MOVED[n]
            eng.wait_ge(s_arc, 63 + 63 - Q * o0)
            for j in range(Q):
                for i in range(Q):
                    if mine(j, i):
                        eng.dma_start(XV[C * i:C * i + C, j, :, o0:o1, :],
                                      XW[C * j:C * j + C, i, :, o0:o1, :]).then_inc(sems[j], 16)

        def move_columns(eng, v0, v1, mine, done):
            k = NW - 1 - v0 // (HO // NW)
            w0 = Q * v0 % WRUN
            eng.wait_ge(s_arc, 3 * 63 + 63 - Q * v0)
            for i in range(Q):
                for bl in range(BL):
                    if mine(i, bl):
                        eng.dma_start(CO[C * bl:C * bl + C, k, i, w0:w0 + Q * (v1 - v0)],
                                      XF[C * i:C * i + C, Q * v0:Q * v1, BH * bl:BH * bl + BH, :]
                                      ).then_inc(done, 16)

        def add_conv(eng, k, bh, done):
            eng.tensor_tensor(X3[:, k, bh], CO[:, k, :, :, bh], by_run(RC[:, TOK * bh:TOK * (bh + 1)], k),
                              ALU.add).then_inc(done, 1)

        block = ctx.enter_context(nc.Block())

        @block.sync
        def _(sp):
            for g in range(8):
                sp.dma_start(RA[:, 1024 * g:1024 * g + 1024], x_in[:, 1024 * g:1024 * g + 1024]).then_inc(s_x[g], 16)
            for c in range(2):
                sp.dma_start(RE[:, WCOLS * c:WCOLS * (c + 1)], wspec[c]).then_inc(s_wc[c], 16)
            for o, i in ((conv_sb, conv_w), (convb_sb, conv_b), (gate_sb, gate_w), (gateb_sb, gate_b),
                         (w2_sb, w2), (b2_sb, b2), (own_sb, own)):
                sp.dma_start(o[:], i).then_inc(s_par, 16)
            sp.dma_start(w1_sb[:], w1[0]).then_inc(s_w1[0], 16)
            for c in range(2, NCH):
                if c == 2:
                    sp.wait_ge(s_sum, 8)
                else:
                    sp.wait_ge(s_mix, 4 * (c - 2))
                sp.dma_start(RE[:, WCOLS * (c % 3):WCOLS * (c % 3 + 1)], wspec[c]).then_inc(s_wc[c % 3], 16)
            sp.wait_ge(s_t0, NCH)
            sp.wait_ge(s_t1, NCH)
            sp.dma_start(RC, x_in).then_inc(s_xr, 16)
            sp.wait_ge(s_h, 1)
            sp.dma_start(w1_sb[:], w1[1]).then_inc(s_w1[1], 16)
            for n in range(len(MOVED)):
                move_rows(sp, n, lambda j, i: n < len(MOVED) - 1 or not on_pool(j, i), s_ph)
            for k in range(3):
                move_columns(sp, 12 - 4 * k, 16 - 4 * k, lambda i, bl: True, s_co[k])
            move_columns(sp, 2, 4, lambda i, bl: True, s_co[3])
            move_columns(sp, 0, 2, lambda i, bl: not on_pool(i, bl), s_co[3])
            for i in range(2 * NW):
                halves = out.rearrange("p (k t a n) -> p k a t n", k=NW, t=BH, a=2)
                done = RA[:, :].rearrange("p (k t a n) -> p k a t n", k=NW, t=BH, a=2)
                sp.wait_ge(s_ad, 16 + 2 * (i + 1))
                sp.dma_start(halves[:, i // 2, i % 2], done[:, i // 2, i % 2]).then_inc(s_out, 16)
            sp.wait_ge(s_out, 16 * 2 * NW)

        @block.gpsimd
        def _(pool):
            pool.memset(RB[:, :], 0.0).then_inc(s_zero, 1)

            def squares(l):
                for g in POOL_GROUPS:
                    pool.wait_ge(s_xc, 8 * l + g + 1)
                    pool.wait_ge(s_sum, EX0[l] + g - 1)
                    xc = centred(l, g)
                    pool.tensor_tensor(square[:, 1, 0:1024], xc, xc, ALU.mult).then_inc(s_sqp, 1)

            squares(0)
            move_rows(pool, len(MOVED) - 1, on_pool, s_php)
            for k in range(NW - 1):
                pool.wait_ge(s_co[k], 16 * Q * BL)
                for bh in range(BH):
                    add_conv(pool, k, bh, s_x3)
            move_columns(pool, 0, 2, on_pool, s_cop)
            squares(1)

        @block.tensor
        def _(pe):
            def group(j, ins, rhs):
                for n, lhs in enumerate(ins):
                    if rhs is None:
                        m = pe.transpose(blk(slot(j), n), lhs, ident)
                    else:
                        m = pe.matmul(blk(slot(j), n), lhs, rhs, start=True, stop=True)
                m.then_inc(s_full, 1)

            def centre_group(ln, g):
                if ln == 0:
                    pe.wait_ge(s_x[g], 16)
                else:
                    pe.wait_ge(s_ad, 2 * g + 2 if g < 2 else 16)
                if g >= 4:
                    pe.wait_ge(s_fd, 8 * ln + g - 3)
                for n in range(8):
                    if ln == 0:
                        src = blk(RA, 8 * g + n)
                    else:
                        first = 1024 * g + BANK * (n // Q)
                        src = RC[:, first + n % Q:first + BANK:Q]
                    m = pe.matmul(blk(ln_slot(g), n), src, centre, start=True, stop=True)
                m.then_inc(s_cen, 1)

            def norm_tokens(ln, follow):
                def follower(g):
                    pe.wait_ge(s_nrm, 8 * ln + g + 1)
                    follow(g).then_inc(s_ff, 1)

                if ln == 1:
                    follower(0)
                for g in range(2 * ln, 4):
                    centre_group(ln, g)
                for g in range(ln, 8):
                    follower(g)
                    if 1 <= g < 5:
                        centre_group(ln, g + 3)

            def keep_warm(bank, n):
                for _ in range(n):
                    pe.matmul(PS[:, bank, 0:P], warm[:, :], warm[:, :], start=True, stop=True)

            pe.wait_ge(s_set, N_SET)
            keep_warm(7, 42)
            pe.wait_ge(s_dft, 16)

            def dft_w(g):
                for n in range(8):
                    m = pe.matmul(blk(ln_slot(g), n), blk(RD, 8 * g + n), fwd_w, start=True, stop=True)
                return m

            norm_tokens(0, dft_w)
            pe.wait_ge(s_fd, 8)
            pe.wait_ge(s_par, 16 * N_PAR)
            for l in range(2):
                m = pe.matmul(PS[:, 6 + l, 0:BL * NE], centre, gate_sb[:, l, :], start=True, stop=True)
            m.then_inc(s_gp, 1)
            for g in range(8):
                if g == 3:
                    pe.wait_ge(s_gpc, 1)
                if g >= 4:
                    wait_one_drained(pe, G_T1 + g - 4)
                group(G_T1 + g, [blk(RC, 8 * g + n) for n in range(8)], None)

            def spectrum(c):
                if c == 0:
                    wait_one_drained(pe, G_T1 + 4)
                    keep_warm(0, 20)
                    wait_drained(pe, G_T1 + 7)
                if c >= 2:
                    pe.wait_ge(s_xbd, c - 1)
                    pe.wait_ge(s_xba, c - 1)
                for bh in range(BH):
                    for y in range(KYC):
                        m = pe.matmul(blk(PS[:, 2 * (c % 2) + bh, :], y), blk(RA, bh * KY + c * KYC + y), fwd_h,
                                      start=True, stop=True)
                m.then_inc(s_f2, 1)

            def mix(c):
                pe.wait_ge(s_xbd, c + 1)
                pe.wait_ge(s_xba, c + 1)
                pe.wait_ge(s_wc[c % 3], 16 * (c // 3 + 1))
                for k in range(4):
                    if c >= 1:
                        pe.wait_ge(s_md if k < 2 else s_ma, 2 * (c - 1) + k % 2 + 1)
                    for n in range(8):
                        x, y = divmod(8 * k + n, KYC)
                        for a in range(2):
                            o = PS[64 * a:64 * a + 64, 4 + k, :].rearrange("p (x w y o) -> p x y w o", x=2, w=2, y=KYC)
                            m = pe.matmul(o[:, x % 2, y],
                                          XB[:, c % 2, x, 2 * y + a].rearrange("p r q b -> p (r q b)"),
                                          WR[:, c % 3, a, x, y, :], start=True, stop=True)
                    m.then_inc(s_mix, 1)

            spectrum(0)
            for c in range(NCH):
                if c + 1 < NCH:
                    spectrum(c + 1)
                if c == 0:
                    keep_warm(7, 30)
                mix(c)

            for c in range(NCH):
                if c == 0:
                    pe.wait_ge(s_xbd, NCH)
                    pe.wait_ge(s_xba, NCH)
                pe.wait_ge(s_md, 2 * NCH if c else 2)
                pe.wait_ge(s_ma, 2 * NCH if c else 2)
                for w, full, read in ((1, s_t1, s_tmp), (0, s_t0, s_comb)):
                    if c >= 2:
                        pe.wait_ge(read, c - 1)
                    for x in range(X8):
                        m = pe.transpose(blk(banks(4 * (c % 2) + 2 * w, 2), x), Z[:, c, x, w], ident)
                    m.then_inc(full, 1)
            pe.wait_ge(s_tmp, NCH - 1)

            def turn(g, ins):
                for n, lhs in enumerate(ins):
                    m = pe.transpose(blk(turn_slot(g), n), lhs, ident)
                m.then_inc(s_tf, 1)

            def turn_spectrum(c):
                pe.wait_ge(s_comb, max(c + 1, NCH - 1))
                if c >= 2:
                    pe.wait_ge(s_td, c - 1)
                turn(c, [V_of_b[:, c, :, b] for b in range(B)])

            def dft_h(g):
                pe.wait_ge(s_td, 2 * (g // 2) + 2)
                if g >= 2:
                    pe.wait_ge(s_dr, g - 1)
                for n in range(8):
                    m = pe.matmul(blk(dft_slot(g), n), blk(RB, KY * (g % 2) + 8 * (g // 2) + n), inv_h,
                                  start=True, stop=True)
                m.then_inc(s_df, 1)

            for c in range(4):
                turn_spectrum(c)
            pe.wait_ge(s_comb, NCH)
            pe.wait_ge(s_tmp, NCH)
            for g in range(8):
                dft_h(g)
                if g % 2 and g < 5:
                    turn_spectrum(g + 3)
                    turn_spectrum(g + 4)

            def turn_image(g):
                if g == 0:
                    pe.wait_ge(s_dr, 7)
                if g == 4:
                    pe.wait_ge(s_dr, 8)
                pe.wait_ge(s_td, 8 + max(g - 1, 0))
                turn(g, [blk(RD, 8 * g + n) for n in range(8)])

            def dft_w_back(g):
                pe.wait_ge(s_td, 8 + g + 1)
                if g < 2:
                    pe.wait_ge(s_dr, 7 + g)
                else:
                    pe.wait_ge(s_res, g - 1)
                for n in range(8):
                    m = pe.matmul(blk(dft_slot(g), n), blk(RB, 8 * g + n), inv_w, start=True, stop=True)
                m.then_inc(s_if1, 1)

            turn_image(0)
            turn_image(1)
            for g in range(8):
                dft_w_back(g)
                if g + 2 < 8:
                    turn_image(g + 2)

            def experts(l):
                if l == 0:
                    pe.wait_ge(s_gpc, 3)
                    pe.wait_ge(s_res, 6)
                    keep_warm(0, 16)
                    pe.wait_ge(s_res, 8)
                if l == 1:
                    pe.wait_ge(s_st, row_count(3, H - 1))
                for g in range(8):
                    if l == 1:
                        if g < 6:
                            pe.wait_ge(s_x3, 2 * (g // 2) + 2)
                        else:
                            pe.wait_ge(s_x3d, g - 5)
                    if g >= 2:
                        pe.wait_ge(s_xc, 8 * l + g - 1)
                    for n in range(8):
                        t, bh = 8 * (g // 2) + n, g % 2
                        src = blk(RC, bh * NT + t) if l == 0 else blk(RA, 8 * g + n)
                        m = pe.matmul(PS[:, 4 * (g % 2) + n // 2, 192 * (n % 2):192 * (n % 2) + 192], src,
                                      proj[:, l, :], start=True, stop=True)
                    m.then_inc(s_pr, 1)
                for g in range(4):
                    pe.wait_ge(s_lg, 8 * l + 2 * g + 2)
                    if g % 2 == 0:
                        pe.wait_ge(s_xc, 8 * l + 7 + g // 2)
                    group(G_LT[l] + g, [LT[:, 8 * g + n].rearrange("p h n -> p (h n)") for n in range(8)], None)
                pe.wait_ge(s_ld, 4 * l + 4)
                keep_warm(0, 110)
                pe.wait_ge(s_rs, l + 1)
                pe.transpose(PS[0:1, 6, 0:P], rsum[:, :], ident).then_inc(s_rt, 1)

                def pool_tokens(g):
                    pe.wait_ge(s_wtd, 4 * l + g + 1)
                    for t in range(8 * g, 8 * g + 8):
                        for bh in range(BH):
                            m = pe.matmul(PS[:, 4 + bh, 0:P], blk(centred(l, 2 * (t // 8) + bh), t % 8), WTOK[:, t, :],
                                          start=(t == 0), stop=(t == NT - 1))
                    return m

                for g in range(4):
                    pe.wait_ge(s_ord if l else s_msk, g + 1)
                    if g >= 2:
                        pe.wait_ge(s_wtd, 4 * l + g - 1)
                    for n in range(8):
                        m = pe.transpose(blk(banks(2 * (g % 2), 2), n), blk(CW[l], 8 * g + n), ident)
                    m.then_inc(s_wt, 1)
                    if g < 2:
                        keep_warm(7, 14)
                    if g == 1:
                        pe.wait_ge(s_rr, l + 1)
                        pe.matmul(PS[0:C, 7, 0:P], ones[:, :], rs_row[:, :], start=True, stop=True).then_inc(s_rb, 1)
                    if g >= 1:
                        pool_tokens(g - 1)
                pool_tokens(3).then_inc(s_pl, 1)
                keep_warm(3, 16)
                pe.wait_ge(s_pc, l + 1)
                pe.wait_ge(s_w1[l], 16)
                for e in range(NE):
                    m = pe.matmul(PS[:, 6, B * e:B * e + B], w1_sb[:, e, :], pooled[:, :, e], start=True, stop=True)
                m.then_inc(s_h, 1)
                keep_warm(3, 8)
                pe.wait_ge(s_g, l + 1)
                for e in range(NE):
                    m = pe.matmul(PS[0:C, 7, B * e:B * e + B], w2_sb[:, l, e, :], hid[:, e, :], start=True, stop=True)
                m.then_inc(s_o, 1)
                keep_warm(3, 8)
                pe.wait_ge(s_ob, l + 1)
                pe.transpose(PS[:, 4, 0:C], eout[:, :, :].rearrange("p b e -> p (b e)"),
                             ident[0:C, 0:C]).then_inc(s_ot, 1)
                keep_warm(3, 10)
                pe.wait_ge(s_os, l + 1)
                for k in range(16):
                    if k >= 4:
                        pe.wait_ge(s_ad, 16 * l + k - 3)
                    if l == 0:
                        bh, ch = divmod(k, 8)
                    else:
                        ch, bh = divmod(k, 2)
                    rhs = CW[l][:, ch * BANK:(ch + 1) * BANK]
                    pe.matmul(PS[:, 4 + k % 4, :], espread[:, BL * bh:BL * bh + BL, :].rearrange("p b o -> p (b o)"), rhs,
                              start=True, stop=True).then_inc(s_sc, 1)
                    if l == 0 and k in FED:
                        centre_group(1, FED.index(k))

            experts(0)

            def turn_rows(g):
                for n in range(8):
                    bl, hb = divmod(n, 2)
                    m = pe.transpose(blk(ln_slot(g), n), blk(RA, 8 * g + BL * hb + bl), ident)
                return m

            norm_tokens(1, turn_rows)

            pe.wait_ge(s_fd, 16)
            for s in range(4):
                def step(q, u):
                    pe.wait_ge(s_st, row_count(s, Q * q + u - 1))
                    for d in range(3):
                        m = pe.matmul(PS[:, u % 2, 0:P].rearrange("p (b v) -> p b v", b=B), conv_sb[:, s, d, :],
                                      state[:, (u + 1 + s) % 2, :, d:d + HO], start=(d == 0), stop=(d == 2))
                    m.then_inc(s_cv, 1)
                    for _ in range(4):
                        pe.matmul(PS[:, 2, 0:P], warm[:, :], warm[:, :], start=True, stop=True)

                for u in range(1, Q):
                    step(0, u)
                with pe.Fori(1, HO) as q:
                    for u in range(Q):
                        step(q, u)

            experts(1)

        @block.scalar
        def _(act):
            act.dma_start(dft_sb[:], dft).then_inc(s_dft, 16)

            def root(n, first, width, eps):
                act.wait_ge(s_sum, n + 1)
                act.activation(std[:, first:first + width], sums[:, first:first + width], ACT.Sqrt, bias=eps,
                               scale=1.0 / C).then_inc(s_std, 1)

            def norm_tokens(ln, pairs):
                def drain_follower(g):
                    act.wait_ge(s_ff, 8 * ln + g + 1)
                    for o, i in pairs(g, ln_slot(g)):
                        m = act.copy(o, i)
                    m.then_inc(s_fd, 1)

                for g in range(8):
                    if g == 4 - 2 * ln:
                        drain_follower(0)
                    if g >= 4:
                        drain_follower(g - 3)
                    act.wait_ge(s_cen, 8 * ln + g + 1)
                    if LN0[ln] + g >= 2:
                        act.wait_ge(s_sum, LN0[ln] + g - 1)
                    act.activation(square[:, g % 2, 0:1024], ln_slot(g), ACT.Square).then_inc(s_sq, 1)
                    if ln == 1 and g < 2:
                        root(LN0[1] + g, 32 * g, 32, eps_sb[:, 0:1])
                    elif g >= 1 + 2 * ln:
                        root(LN0[ln] + g - 1, 32 * (g - 1), 32, eps_sb[:, 0:1])
                root(LN0[ln] + 7, 224, 32, eps_sb[:, 0:1])
                for g in range(5, 8):
                    drain_follower(g)

            def drain(j, pairs):
                act.wait_ge(s_full, j + 1)
                for o, i in pairs(j):
                    m = act.copy(o, i)
                m.then_inc(s_da, 1)

            act.wait_ge(s_set, N_SET)
            norm_tokens(0, f1_pairs)
            for j in range(G_T1, G_T1 + 8, 2):
                drain(j, t1_pairs)

            def spread(c):
                act.wait_ge(s_f2, c + 1)
                if c == 0:
                    act.wait_ge(s_zero, 1)
                if c >= 2:
                    act.wait_ge(s_mix, 4 * (c - 1))
                for o, i in xb_pairs(c, 1):
                    m = act.copy(o, i)
                m.then_inc(s_xba, 1)

            spread(0)
            for c in range(NCH):
                if c + 1 < NCH:
                    spread(c + 1)
                for k in (2, 3):
                    act.wait_ge(s_mix, 4 * c + k + 1)
                    act.copy(z_bank(c, k), PS[:, 4 + k, :]).then_inc(s_ma, 1)
            for c in range(NCH):
                act.wait_ge(s_t1, c + 1)
                if c >= 2:
                    act.wait_ge(s_comb, c - 1)
                act.copy(imtmp[:, c % 2, :], banks(4 * (c % 2) + 2, 2)).then_inc(s_tmp, 1)
            for first, pairs in ((0, t2_pairs), (8, t3_pairs)):
                for g in range(8):
                    act.wait_ge(s_tf, first + g + 1)
                    for o, i in pairs(g):
                        m = act.copy(o, i)
                    m.then_inc(s_td, 1)

            def experts(l):
                for g in range(8):
                    act.wait_ge(s_pr, 8 * l + g + 1)
                    xc = PS[:, 4 * (g % 2):4 * (g % 2) + 4, 0:384].rearrange("p k (j n) -> p k j n", j=2)[:, :, :, 0:P]
                    t0, bh = 8 * (g // 2), g % 2
                    raw = PS[:, 4 * (g % 2):4 * (g % 2) + 4, 0:384].rearrange("p k (j n) -> p k j n", j=2)[:, :, :, P:]
                    act.copy(LT[:, t0:t0 + 8, bh, :].rearrange("p (k j) n -> p k j n", j=2), raw)
                    if g not in POOL_GROUPS:
                        act.wait_ge(s_sum, EX0[l] + g - 1)
                        act.activation(square[:, g % 2, 0:1024].rearrange("p (k j n) -> p k j n", k=4, j=2), xc,
                                       ACT.Square).then_inc(s_sq, 1)
                    act.copy(centred(l, g).rearrange("p (k j n) -> p k j n", k=4, j=2), xc).then_inc(s_xc, 1)
                    if g >= 1:
                        root(EX0[l] + g - 1, 32 * (g - 1), 32, eps_sb[:, 1:2])
                root(EX0[l] + 7, 224, 32, eps_sb[:, 1:2])
                for j in range(G_LT[l], G_LT[l] + 4):
                    act.wait_ge(s_full, j + 1)
                    o, i = lt_pair(l, j)
                    act.activation(o, i, ACT.Identity, bias=gateb_sb[:, l:l + 1]).then_inc(s_ld, 1)
                act.wait_ge(s_nm, l + 1)
                act.activation(E, L[l], ACT.Exp, bias=negmax[:, :], accum_out=expsum[:, :]).then_inc(s_exp, 1)
                if l == 1:
                    for k in range(NW):
                        act.wait_ge(s_msk, 4 + k + 1)
                        act.copy(CW[1][:, 1024 * k:1024 * k + 1024].rearrange("p (i w o) -> p i w o", i=Q, w=WRUN),
                                 by_run(E, k)).then_inc(s_ord, 1)
                act.wait_ge(s_rt, l + 1)
                act.copy(rs_row[:, :], PS[0:1, 6, 0:P]).then_inc(s_rr, 1)
                act.wait_ge(s_rb, l + 1)
                act.copy(rs_rep[:, :], PS[0:C, 7, 0:P]).then_inc(s_rp, 1)
                act.wait_ge(s_h, l + 1)
                act.activation(hid[:, :, :].rearrange("p e b -> p (e b)"), PS[:, 6, 0:P], ACT.Gelu).then_inc(s_g, 1)

            act.wait_ge(s_par, 16 * N_PAR)
            experts(0)

            norm_tokens(1, xw_pairs)

            for s in range(4):
                def fetch(s, q, u):
                    act.activation(rowb[:, u], row_at(SRC[s], s, q, u), ACT.Identity,
                                   bias=convb_sb[:, s:s + 1]).then_inc(s_row, 1)

                def archive(q, u):
                    act.copy(row_at(DST[s], s, q, u), state[:, (u + s) % 2, :, 1:1 + HO]).then_inc(s_arc, 1)

                def step(q, u):
                    act.wait_ge(s_st, row_count(s, Q * q + u))
                    fetch(s, q + (u + 1) // Q, (u + 1) % Q)
                    archive(q, u)

                if s == 0:
                    act.wait_ge(s_fd, 16)
                    fetch(s, 0, 1)
                elif s == 2:
                    wait_columns(act, 0)
                    act.copy(XF[:, 0], XV[:, 0, :, :, 0])
                    wait_columns(act, 1)
                    fetch(s, 0, 1)
                for u in range(1, Q):
                    if s == 2 and u < Q - 1:
                        wait_columns(act, u + 1)
                    step(0, u)
                with act.Fori(1, HO - 1) as q:
                    for u in range(Q):
                        step(q, u)
                for u in range(Q - 1):
                    step(HO - 1, u)
                act.wait_ge(s_st, row_count(s, H - 1))
                if s % 2 == 0:
                    act.wait_ge(s_arc, 63 * s + 62)
                    fetch(s + 1, 0, 1)
                archive(HO - 1, Q - 1)

            experts(1)

        @block.vector
        def _(dve):
            dve.memset(eps_sb[:, 0:1], LN_C_EPS[0]).then_inc(s_set, 1)
            dve.memset(eps_sb[:, 1:2], LN_T_EPS).then_inc(s_set, 1)
            dve.memset(state[:, :, :, :], 0.0).then_inc(s_set, 1)
            dve.memset(ones[:, :], 1.0).then_inc(s_set, 1)
            dve.memset(pooled[C:C + 1, :, :], 1.0).then_inc(s_set, 1)
            dve.memset(warm[:, :], 0.0).then_inc(s_set, 1)

            def norm_tokens(ln):
                def total(g):
                    dve.wait_ge(s_sq, LNS[ln] + g + 1)
                    dve.tensor_reduce(sums[:, 32 * g:32 * g + 32],
                                      square[:, g % 2, 0:1024].rearrange("p (a c) -> p a c", c=C), AX_X,
                                      ALU.add).then_inc(s_sum, 1)

                def norm(g):
                    r = rstd[:, 32 * g:32 * g + 32]
                    dve.wait_ge(s_std, LN0[ln] + g + 1)
                    dve.reciprocal(r, std[:, 32 * g:32 * g + 32]).then_inc(s_rec, 1)
                    dve.wait_ge(s_rec, LN0[ln] + g + 1)
                    if ln == 0:
                        m = dve.tensor_tensor(RD[:, 1024 * g:1024 * g + 1024].rearrange("p (a c) -> p a c", c=C),
                                              ln_slot(g).rearrange("p (a c) -> p a c", c=C),
                                              r.unsqueeze(2).to_broadcast([P, 32, C]), ALU.mult)
                    else:
                        for hb in range(2):
                            k = slice(BANK * hb, BANK * (hb + 1))
                            m = dve.tensor_tensor(
                                RA[:, 1024 * g:1024 * g + 1024][:, k].rearrange("p (b j c) -> p j b c", b=BL, j=Q),
                                ln_slot(g)[:, k].rearrange("p (j b c) -> p j b c", b=BL, j=Q),
                                r[:, 16 * hb:16 * hb + 16].rearrange("p (j b) -> p j b", b=BL).unsqueeze(3)
                                .to_broadcast([P, Q, BL, C]), ALU.mult)
                    m.then_inc(s_nrm, 1)

                def add_experts(first, last):
                    for k in range(first, last):
                        x2 = RC[:, BANK * k:BANK * (k + 1)]
                        dve.wait_ge(s_sc, k + 1)
                        dve.tensor_tensor(x2, PS[:, 4 + k % 4, :], x2, ALU.add).then_inc(s_ad, 1)

                if ln == 0:
                    total(0)
                    total(1)
                    norm(0)
                    total(2)
                    norm(1)
                    total(3)
                    norm(2)
                else:
                    add_experts(0, FED[0] + 1)
                    total(0)
                    add_experts(FED[0] + 1, FED[1] + 1)
                    norm(0)
                    total(1)
                    add_experts(FED[1] + 1, 16)
                    norm(1)
                    total(2)
                    total(3)
                    norm(2)
                for g in range(3, 8):
                    if g < 7:
                        total(g + 1)
                    norm(g)

            def drain(j, pairs):
                dve.wait_ge(s_full, j + 1)
                for o, i in pairs(j):
                    m = dve.tensor_copy(o, i)
                m.then_inc(s_dd, 1)

            norm_tokens(0)
            dve.wait_ge(s_gp, 1)
            dve.tensor_copy(proj[:, :, P:], PS[:, 6:8, 0:BL * NE]).then_inc(s_gpc, 1)
            for j in range(G_T1 + 1, G_T1 + 8, 2):
                drain(j, t1_pairs)

            def spread(c):
                dve.wait_ge(s_f2, c + 1)
                if c == 0:
                    dve.wait_ge(s_zero, 1)
                if c >= 2:
                    dve.wait_ge(s_mix, 4 * (c - 1))
                for o, i in xb_pairs(c, 0):
                    m = dve.tensor_copy(o, i)
                m.then_inc(s_xbd, 1)

            spread(0)
            for c in range(NCH):
                if c + 1 < NCH:
                    spread(c + 1)
                for k in (0, 1):
                    dve.wait_ge(s_mix, 4 * c + k + 1)
                    dve.tensor_copy(z_bank(c, k), PS[:, 4 + k, :]).then_inc(s_md, 1)
            dve.tensor_scalar(negb_sb[:, :], convb_sb[:, :], -1.0, None, ALU.mult).then_inc(s_gpc, 1)
            dve.tensor_copy(proj[:, :, 0:P], centre.unsqueeze(1).to_broadcast([P, 2, P])).then_inc(s_gpc, 1)
            for c in range(NCH):
                dve.wait_ge(s_t0, c + 1)
                dve.wait_ge(s_tmp, c + 1)
                by_re = banks(4 * (c % 2), 2).rearrange("p (x a r n) -> p x a r n", x=X8, a=2, r=2)
                by_im = imtmp[:, c % 2, :].rearrange("p (x a r n) -> p x a r n", x=X8, a=2, r=2)
                dve.tensor_tensor(V[:, c, :, :, 0, :], by_re[:, :, :, 0, :], by_im[:, :, :, 1, :], ALU.subtract)
                dve.tensor_tensor(V[:, c, :, :, 1, :], by_re[:, :, :, 1, :], by_im[:, :, :, 0, :],
                                  ALU.add).then_inc(s_comb, 1)
            for g in range(8):
                dve.wait_ge(s_df, g + 1)
                for o, i in if2_pairs(g):
                    m = dve.tensor_copy(o, i)
                m.then_inc(s_dr, 1)
            dve.wait_ge(s_xr, 16)
            for g in range(8):
                dve.wait_ge(s_if1, g + 1)
                x1 = RC[:, 1024 * g:1024 * g + 1024]
                dve.tensor_tensor(x1, dft_slot(g), x1, ALU.add).then_inc(s_res, 1)

            def experts(l):
                def total(g):
                    if g in POOL_GROUPS:
                        dve.wait_ge(s_sqp, 3 * l + g // 2 + 1)
                    else:
                        dve.wait_ge(s_sq, EXS[l] + (g + 1) // 2 + 1)
                    dve.tensor_reduce(sums[:, 32 * g:32 * g + 32],
                                      square[:, g % 2, 0:1024].rearrange("p (a c) -> p a c", c=C), AX_X,
                                      ALU.add).then_inc(s_sum, 1)

                def scale(g):
                    t0, bh = 8 * (g // 2), g % 2
                    r = rstd[:, :].rearrange("p (t h b) -> p h t b", h=BH, b=BL)[:, bh, t0:t0 + 8, :]
                    dve.wait_ge(s_std, EX0[l] + g + 1)
                    dve.reciprocal(r, std[:, 32 * g:32 * g + 32].rearrange("p (t b) -> p t b", b=BL)
                                   ).then_inc(s_rec, 1)
                    dve.wait_ge(s_rec, EX0[l] + g + 1)
                    lt = LT[:, t0:t0 + 8, bh, :].rearrange("p t (b e) -> p t b e", e=NE)
                    dve.tensor_tensor(lt, lt, r.unsqueeze(3).to_broadcast([P, 8, BL, NE]), ALU.mult).then_inc(s_lg, 1)

                total(0)
                if l == 1:
                    share = sum(on_pool(i, bl) for i in range(Q) for bl in range(BL))
                    dve.wait_ge(s_cop, 16 * share)
                    dve.wait_ge(s_co[NW - 1], 16 * (2 * Q * BL - share))
                    add_conv(dve, NW - 1, 0, s_x3d)
                for g in range(8):
                    if g < 7:
                        total(g + 1)
                    scale(g)
                    if l == 1 and g == 1:
                        add_conv(dve, NW - 1, 1, s_x3d)
                for g in range(4):
                    dve.wait_ge(s_ld, 4 * l + g + 1)
                    dve.max(cand[:, 8 * g:8 * g + 8], part(L[l], l, g)).then_inc(s_pm, 1)
                dve.wait_ge(s_pm, 4 * l + 4)
                dve.max(top8[:, :], cand[:, :]).then_inc(s_mx, 1)
                dve.wait_ge(s_mx, l + 1)
                dve.tensor_scalar(negmax[:, :], top8[:, 0:1], -1.0, None, ALU.mult).then_inc(s_nm, 1)
                dve.match_replace(L2, top8[:, :], L[l], MASKED).then_inc(s_rep, 1)
                dve.wait_ge(s_exp, l + 1)
                dve.reciprocal(rsum[:, :], expsum[:, :]).then_inc(s_rs, 1)
                dve.wait_ge(s_rep, l + 1)
                def mask(g):
                    left, chosen = (part(x, l, g) for x in (L2, E))
                    dve.scalar_tensor_tensor(out=chosen, in0=left, scalar=MASKED / 2, in1=chosen,
                                             op0=ALU.is_le, op1=ALU.mult).then_inc(s_msk, 1)

                def weigh(g):
                    dve.wait_ge(s_wt, 4 * l + g + 1)
                    dve.tensor_tensor(WTOK[:, 8 * g:8 * g + 8, :].rearrange("p t (b e) -> p (t b) e", e=NE),
                                      banks(2 * (g % 2), 2).rearrange("p (a e) -> p a e", e=NE),
                                      rstd[:, 64 * g:64 * g + 64].unsqueeze(2).to_broadcast([P, 64, NE]),
                                      ALU.mult).then_inc(s_wtd, 1)

                mask(0)
                mask(1)
                if l == 1:
                    mask(2)
                    mask(3)
                weigh(0)
                if l == 0:
                    mask(2)
                weigh(1)
                if l == 0:
                    mask(3)
                weigh(2)
                weigh(3)
                dve.wait_ge(s_pl, l + 1)
                dve.wait_ge(s_rp, l + 1)
                for b in range(B):
                    bh, bl = divmod(b, BL)
                    m = dve.tensor_tensor(pooled[0:C, b, :], PS[C * bl:C * bl + C, 4 + bh, NE * b:NE * b + NE],
                                          rs_rep[:, NE * b:NE * b + NE], ALU.mult)
                m.then_inc(s_pc, 1)
                dve.wait_ge(s_o, l + 1)
                dve.tensor_tensor(eout[:, :, :].rearrange("p b e -> p e b"),
                                  PS[0:C, 7, 0:P].rearrange("p (e b) -> p e b", b=B),
                                  b2_sb[:, l, :].unsqueeze(2).to_broadcast([C, NE, B]), ALU.add).then_inc(s_ob, 1)
                dve.wait_ge(s_ot, l + 1)
                dve.scalar_tensor_tensor(out=espread[:, :, :],
                                         in0=PS[:, 4, 0:C].unsqueeze(1).to_broadcast([P, B, C]),
                                         scalar=rsum[:, :], in1=own_sb[:, :].unsqueeze(2).to_broadcast([P, B, C]),
                                         op0=ALU.mult, op1=ALU.mult).then_inc(s_os, 1)
                if l == 1:
                    for k in range(16):
                        dve.wait_ge(s_sc, 16 + k + 1)
                        run, half, bh = k // 4, k // 2 % 2, k % 2
                        x4 = RA[:, 2048 * run + 1024 * bh + BANK * half:2048 * run + 1024 * bh + BANK * (half + 1)]
                        dve.tensor_tensor(x4, PS[:, 4 + k % 4, :], x4, ALU.add).then_inc(s_ad, 1)

            experts(0)

            norm_tokens(1)

            for s in range(4):
                if s % 2 == 0:
                    if s == 0:
                        dve.wait_ge(s_fd, 16)
                    else:
                        wait_columns(dve, 0)
                    dve.tensor_copy(state[:, 0, :, 1:1 + HO], row_at(SRC[s], s, 0, 0)).then_inc(s_st, 1)

                def step(q, u):
                    dve.wait_ge(s_cv, 63 * s + Q * q + u)
                    dve.wait_ge(s_row, 63 * s + Q * q + u)
                    dve.scalar_tensor_tensor(out=state[:, (u + s) % 2, :, 1:1 + HO],
                                             in0=PS[:, u % 2, 0:P].rearrange("p (b v) -> p b v", b=B),
                                             scalar=negb_sb[:, s:s + 1], in1=rowb[:, u],
                                             op0=ALU.max, op1=ALU.add).then_inc(s_st, 1)

                for u in range(1, Q):
                    step(0, u)
                with dve.Fori(1, HO) as q:
                    for u in range(Q):
                        step(q, u)

            experts(1)


def dft_tables():
    f = np.float64
    centre = np.eye(P, dtype=f) - np.kron(np.eye(BL), np.full((C, C), 1.0 / C))
    w, ky = np.arange(W), np.arange(KY)
    a = 2 * np.pi * np.outer(w, ky) / W
    fwd_w = np.kron(np.eye(2), np.concatenate([np.cos(a), -np.sin(a)], 1) / W)
    h, kx = np.arange(H), np.arange(H)
    a = 2 * np.pi * np.outer(h, kx) / H
    c, s = np.cos(a), np.sin(a)
    full = np.array([[c, -s], [s, c]]) / H
    fwd_h = full.transpose(0, 2, 3, 1).reshape(2, H, 2, Q, X8, 2)
    fwd_h = fwd_h.transpose(0, 1, 2, 3, 5, 4).reshape(P, P)
    inv = np.array([[c, s], [-s, c]])
    inv_h = inv.transpose(3, 0, 1, 2).reshape(2, Q, X8, 2, 2, H)
    inv_h = inv_h.transpose(2, 0, 3, 1, 4, 5).reshape(P, P)
    a = 2 * np.pi * np.outer(ky, w) / W
    twice = np.where(ky == 0, 1.0, 2.0)[:, None]
    inv_w = np.kron(np.eye(2), np.concatenate([twice * np.cos(a), -twice * np.sin(a)], 0))
    return np.ascontiguousarray(np.stack([centre, np.eye(P), fwd_w, fwd_h, inv_h, inv_w], 1).astype(np.float32))


def banded(w):
    m = np.zeros((Q, C, 3, Q, C), w.dtype)
    for d in range(3):
        for i in range(Q):
            for j in range(Q):
                k = Q * (d - 1) + i - j + TAPS // 2
                if 0 <= k < TAPS:
                    m[i, :, d, j, :] = w[:, :, k].T
    return m.reshape(P, 3, P)


def kernel(**inputs):
    import concourse.bacc as bacc
    from concourse.bass_utils import run_bass_kernel_spmd

    a = {k: np.asarray(v) for k, v in inputs.items()}
    x = a["x"].reshape(BH, BL, C, TOK).transpose(1, 2, 0, 3).reshape(P, NF)
    ws = np.stack([np.stack([a[f"L0_conv_w{n}_{p}"] for p in ("real", "imag")]) for n in (1, 2)])
    ws = ws.reshape(2, 2, C, C, Q, X8, NCH, KYC).transpose(6, 4, 2, 0, 5, 7, 1, 3).reshape(NCH, P, WCOLS)
    conv_w = np.stack([banded(a[f"L1_conv_w_{s}"]) for s in "durl"], 1)
    conv_b = np.stack([np.tile(a[f"L1_conv_b_{s}"], Q) for s in "durl"], 1)
    gate = np.zeros((BL, C, 2, BL, NE), np.float32)
    for l in range(2):
        for b in range(BL):
            gate[b, :, l, b, :] = a[f"L{l}_ffn_gate_w"].T
    gate_b = np.stack([np.tile(a[f"L{l}_ffn_gate_b"], B) for l in range(2)], 1)
    w1 = np.stack([a[f"L{l}_ffn_weight1"].transpose(1, 0, 2) for l in range(2)])
    w2 = np.stack([a[f"L{l}_ffn_weight2"][:, :NHID].transpose(1, 0, 2) for l in range(2)], 1)
    b2 = np.stack([a[f"L{l}_ffn_weight2"][:, NHID].T for l in range(2)], 1)
    own = np.repeat(np.eye(B, dtype=np.float32), NE, 0)
    arrays = {"x_in": x, "dft": dft_tables(), "wspec": ws, "conv_w": conv_w, "conv_b": conv_b,
              "gate_w": gate.reshape(P, 2, BL * NE), "gate_b": gate_b, "w1": w1, "w2": w2, "b2": b2, "own": own}
    arrays = {k: np.ascontiguousarray(v) for k, v in arrays.items()}

    nc = bacc.Bacc("TRN2", target_bir_lowering=False, num_devices=1)
    args = [nc.dram_tensor(k, v.shape, F32, kind="ExternalInput").ap() for k, v in arrays.items()]
    args.append(nc.dram_tensor("out", (P, NF), F32, kind="ExternalOutput").ap())
    build_kernel(nc, *args)
    r = run_bass_kernel_spmd(nc, [arrays], core_ids=[0])
    y = np.asarray(r.results[0]["out"])
    y = y.reshape(BL, C, NW, BH, Q, WRUN, HO)[:, :, ::-1].transpose(3, 0, 1, 6, 4, 2, 5)
    return np.ascontiguousarray(y.reshape(B, C, H, W))
```
